# Optimizing a Trainium2 kernel written in Bass

```python
import numpy as np
import jax
import jax.numpy as jnp

def _softmax(x, axis=-1):
    return jax.nn.softmax(x, axis=axis)

def _gelu(x):
    return jax.nn.gelu(x, approximate=True)

def _silu(x):
    return jax.nn.silu(x)

def _sigmoid(x):
    return jax.nn.sigmoid(x)

def _layernorm(x, axis=-1, eps=1e-05):
    m = jnp.mean(x, axis=axis, keepdims=True)
    v = jnp.var(x, axis=axis, keepdims=True)
    return (x - m) / jnp.sqrt(v + eps)

def _scatter_add(tgt, idx, src, axis=0):
    return tgt.at[idx].add(src)

def _segment_sum(src, seg, n):
    return jax.ops.segment_sum(src, seg, n)
kernel_name = 'mk_gnn_preln_d1_gnn_r8_00ccca'

def setup_inputs(seed: int=0):
    np.random.seed(seed)
    _w = jnp.asarray

    def _rec_inputs():
        import jax
        import jax.numpy as jnp
        _gk = jax.random.key(seed)
        x = -0.0003713 + 1 * jax.random.normal(jax.random.fold_in(_gk, 1), (6250, 256), jnp.float32)
        _s = jax.random.randint(jax.random.fold_in(_gk, 2), (50000,), 0, 6250, jnp.int32)
        _d = jax.random.randint(jax.random.fold_in(_gk, 3), (50000,), 0, 6250, jnp.int32)
        _loop = jnp.arange(6250, dtype=jnp.int32)
        src = jnp.concatenate([_s, _d, _loop])
        dst = jnp.concatenate([_d, _s, _loop])
        _o = jnp.argsort(dst, stable=True)
        src = src[_o]
        dst = dst[_o]
        edge_attr_64 = -9.77346e-05 + 0.999888 * jax.random.normal(jax.random.fold_in(_gk, 12), (106250, 64), jnp.float32)
        return (x, src, dst, edge_attr_64)
    x, src, dst, edge_attr_64 = _rec_inputs()

    def _L0_gnn_setup():
        import jax, jax.numpy as jnp
        import numpy as np
        ALPHA = 0.2
        key = jax.random.key(seed)
        ks = jax.random.split(key, 6)
        N, E, F_IN, F_OUT, E_DIM = (6250, 100000, 256, 256, 64)
        h = jax.random.normal(ks[0], (N, F_IN), dtype=jnp.float32)
        e_feat = jax.random.normal(ks[1], (E, E_DIM), dtype=jnp.float32)
        W = jax.random.normal(ks[2], (F_OUT, F_IN), dtype=jnp.float32) * (1.0 / np.sqrt(F_IN))
        A = jax.random.normal(ks[3], (1, 2 * F_OUT + E_DIM), dtype=jnp.float32) * 0.05
        src = jax.random.randint(ks[4], (E,), 0, N, dtype=jnp.int32)
        dst = jax.random.randint(ks[5], (E,), 0, N, dtype=jnp.int32)
        return {'h': h, 'e_feat': e_feat, 'W': W, 'A': A, 'src': src, 'dst': dst}
    _L0_gnn_all = _L0_gnn_setup()
    _L0_gnn_in = {k: v for k, v in _L0_gnn_all.items() if k in ('W', 'A')}
    del _L0_gnn_all
    return {'x': x, 'src': src, 'dst': dst, 'edge_attr_64': edge_attr_64, 'L0_gnn_W': _L0_gnn_in['W'], 'L0_gnn_A': _L0_gnn_in['A']}

def reference(x, src, dst, edge_attr_64, L0_gnn_W, L0_gnn_A):
    import jax
    import jax.numpy as jnp

    def _L0_gnn_ref(h, e_feat, W, A, src, dst):
        import jax, jax.numpy as jnp
        import numpy as np
        ALPHA = 0.2
        N = h.shape[0]
        F_OUT = W.shape[0]
        z = h @ W.T
        z_src = z[src]
        z_dst = z[dst]
        a_src, a_dst, a_e = (A[0, :F_OUT], A[0, F_OUT:2 * F_OUT], A[0, 2 * F_OUT:])
        logits = z_src @ a_src + z_dst @ a_dst + e_feat @ a_e
        e = jax.nn.leaky_relu(logits, ALPHA)
        m = jax.ops.segment_max(e, dst, num_segments=N)
        ex = jnp.exp(e - m[dst])
        denom = jax.ops.segment_sum(ex, dst, num_segments=N)
        alpha = ex / denom[dst]
        h_out = jax.ops.segment_sum(alpha[:, None] * z_src, dst, num_segments=N)
        return h_out
    h = jnp.maximum(_layernorm(x, axis=-1), 0.0)
    x = x + _L0_gnn_ref(h, edge_attr_64, L0_gnn_W, L0_gnn_A, src, dst)
    return x

_drawn_inputs = setup_inputs


def setup_inputs(seed=0):
    import zlib

    import numpy as np

    out = dict(_drawn_inputs(seed))
    spreads = {}
    factors = {}
    for name, (base, spread) in spreads.items():
        noise = np.random.default_rng([zlib.crc32(name.encode()), seed]).standard_normal(out[name].shape)
        drawn = base * np.exp(spread * noise) if base else spread * noise
        out[name] = jnp.asarray(drawn.astype(out[name].dtype))
    for name, factor in factors.items():
        out[name] = (out[name] * factor).astype(out[name].dtype)
    return out
```

```python
from contextlib import ExitStack

import concourse.bass as bass
from concourse import mybir
from concourse.alu_op_type import AluOpType as ALU

ACT = mybir.ActivationFunctionType
F32 = mybir.dt.float32
BF16 = mybir.dt.bfloat16
I32 = mybir.dt.int32
I16 = mybir.dt.int16
AX = mybir.AxisListType

SLOPE = 0.2
EPS = 1e-5
BIG = 2.0 ** 100
TINY = 1e-30


def on_row(table, index_column):
    return dict(in_=table, in_offset=bass.IndirectOffsetOnAxis(ap=index_column, axis=0), out_offset=None)


def gnn_kernel(nc, x, src, dst, edge_attr, W, A, out):
    N, F = x.shape
    E, FE = edge_attr.shape
    WN = CH = 125
    NW, NC = N // WN, E // CH
    assert N == NW * WN and E == NC * CH and F == 256
    KF = F // 128
    ONE, S, ROW = F, F + 1, F + 2
    NT, GRP = 10, 5
    NS = NW // NT
    ST = F + 3

    table = nc.dram_tensor("node_table", (N, ROW), F32).ap()
    state = nc.dram_tensor("node_state", (N, ST), F32).ap()

    with ExitStack() as top:
        def sb(name, shape, dt, where=top):
            return where.enter_context(nc.sbuf_tensor(name, shape, dt))

        def ps(name, shape, where=top):
            return where.enter_context(nc.psum_tensor(name, shape, F32))

        def sem(name, where=top):
            return where.enter_context(nc.semaphore(name))

        x_all = sb("x_all", [WN, NW, F], F32)
        d_all = sb("d_all", [WN, NW], F32)
        ae_bc = sb("ae_bc", [WN, FE], F32)
        WT = sb("WT", [128, KF, F], F32)
        ident = sb("ident", [128, 128], F32)

        with ExitStack() as ctx:
            hs = sb("hs", [WN, NT, ROW], F32, ctx)
            w_sb = sb("w_sb", [128, KF, F], F32, ctx)
            a_col = sb("a_col", [128, 2 * KF], F32, ctx)
            a_rep = sb("a_rep", [128, 2 * KF, WN], F32, ctx)
            ones = sb("ones", [128, 128], F32, ctx)
            uv = sb("uv", [WN, 2, F], F32, ctx)
            stats = sb("stats", [WN, NT, 6], F32, ctx)
            nt = {k: sb(f"nt_{k}", [WN, NT], F32, ctx) for k in (
                "sum", "gap", "sq", "gap2", "sq_all", "var", "std", "inv", "inv2", "ratio", "step", "rstd", "shift")}
            dots = sb("dots", [WN, 2, NT], F32, ctx)
            junk = sb("junk", [WN, 2, F], F32, ctx)
            uv_ps = ps("uv_ps", [WN, 2, F], ctx)
            wt_ps = ps("wt_ps", [128, KF, KF, 128], ctx)

            weights_in = sem("weights_in", ctx)
            x_in = [sem(f"x_in{j}", ctx) for j in range(2)]
            ident_made = sem("ident_made", ctx)
            a_rep_made = sem("a_rep_made", ctx)
            uv_summed = sem("uv_summed", ctx)
            uv_kept = sem("uv_kept", ctx)
            wt_turned = sem("wt_turned", ctx)
            wt_kept = sem("wt_kept", ctx)
            chain = sem("chain", ctx)
            stat_done = sem("stat_done", ctx)
            var_made = sem("var_made", ctx)
            std_made = sem("std_made", ctx)
            shift_made = sem("shift_made", ctx)
            h_made = sem("h_made", ctx)
            dots_done = sem("dots_done", ctx)
            s_kept = sem("s_kept", ctx)
            table_out = [sem(f"table_out{j}", ctx) for j in range(2)]

            x_tiles = x.rearrange("(t p) f -> p t f", p=WN)
            table_tiles = table.rearrange("(t p) f -> p t f", p=WN)

            with nc.Block() as block:
                @block.sync
                def _(sp):
                    sp.dma_start(w_sb[:], W.rearrange("(c p) i -> p c i", p=128)).then_inc(weights_in, 16)
                    sp.dma_start(a_col[:], A[0, 0:2 * F].rearrange("(c p) -> p c", p=128), allow_slow_non_contiguous=True).then_inc(weights_in, 16)
                    sp.dma_start(ae_bc[:], A[0, 2 * F:2 * F + FE].partition_broadcast(WN)).then_inc(weights_in, 16)

                @block.gpsimd
                def _(pool):
                    with pool.Fori(0, NS) as i:
                        for j in range(2):
                            pool.wait_ge(x_in[j], 16 * i)
                            t = bass.ds(NT * i + GRP * j, GRP)
                            pool.dma_start(x_all[:, t, :], x_tiles[:, t, :]).then_inc(x_in[j], 16)
                    nc.gpsimd.memset(ident[:], 0.0).then_inc(ident_made, 1)
                    pool.wait_ge(ident_made, 1)
                    nc.gpsimd.affine_select(out=ident[:], in_=ident[:], compare_op=ALU.not_equal, fill=1.0, base=0,
                                            pattern=[[-1, 128]], channel_multiplier=1).then_inc(ident_made, 1)
                    with pool.Fori(0, NS) as i:
                        for j in range(2):
                            pool.wait_ge(s_kept, 2 * i + j + 1)
                            pool.dma_start(table_tiles[:, bass.ds(NT * i + GRP * j, GRP), :],
                                           hs[:, GRP * j:GRP * j + GRP, :]).then_inc(table_out[j], 16)
                    for j in range(2):
                        pool.wait_ge(table_out[j], 16 * NS)

                @block.tensor
                def _(pe):
                    pe.wait_ge(ident_made, 2)
                    pe.wait_ge(weights_in, 48)
                    for a in range(KF):
                        for b in range(KF):
                            mm = nc.tensor.transpose(wt_ps[:, a, b, :], w_sb[:, b, 128 * a:128 * a + 128], ident[:])
                    mm.then_inc(wt_turned, 1)
                    pe.wait_ge(a_rep_made, 2 * KF)
                    for s in range(2):
                        for c in range(KF):
                            mm = nc.tensor.matmul(uv_ps[:, s, :], a_rep[:, KF * s + c, :], w_sb[:, c, :],
                                                  start=(c == 0), stop=(c == KF - 1))
                    mm.then_inc(uv_summed, 1)

                @block.scalar
                def _(act):
                    act.wait_ge(wt_turned, 1)
                    nc.scalar.copy(WT[:].rearrange("p a f -> p (a f)"),
                                   wt_ps[:].rearrange("p a b f -> p (a b f)")).then_inc(wt_kept, 1)
                    with act.Fori(0, NS) as i:
                        act.wait_ge(var_made, i + 1)
                        nc.scalar.activation(nt["std"][:], nt["var"][:], ACT.Sqrt).then_inc(std_made, 1)
                        act.wait_ge(shift_made, i + 1)
                        for j in range(NT):
                            if j % GRP == 0:
                                act.wait_ge(table_out[j // GRP], 16 * i)
                            nc.scalar.activation(hs[:, j, 0:F], x_all[:, bass.ds(NT * i + j, 1), :], ACT.Relu,
                                                 bias=nt["shift"][:, j:j + 1],
                                                 scale=nt["rstd"][:, j:j + 1]).then_inc(h_made, 1)

                @block.vector
                def _(dve):
                    nc.vector.memset(ones[:], 1.0).then_inc(chain, 1)
                    nc.vector.memset(hs[:, :, ONE], 1.0).then_inc(chain, 1)
                    dve.wait_ge(chain, 2)
                    dve.wait_ge(weights_in, 48)
                    for c in range(2 * KF):
                        nc.vector.tensor_scalar(a_rep[:, c, :], ones[:, 0:WN], a_col[:, c:c + 1], None,
                                                ALU.mult).then_inc(a_rep_made, 1)
                    dve.wait_ge(uv_summed, 1)
                    nc.vector.tensor_copy(uv[:], uv_ps[:]).then_inc(uv_kept, 1)
                    dve.wait_ge(uv_kept, 1)
                    links = 10
                    with dve.Fori(0, NS) as i:
                        for j in range(NT):
                            if j % GRP == 0:
                                dve.wait_ge(x_in[j // GRP], 16 * i + 16)
                            nc.vector.bn_stats(stats[:, j, :], x_all[:, bass.ds(NT * i + j, 1), :]
                                               .rearrange("p a f -> p (a f)")).then_inc(stat_done, 1)
                        dve.wait_ge(stat_done, NT * i + NT)
                        n = [2]

                        def then(ins):
                            n[0] += 1
                            ins.then_inc(chain, 1)
                            dve.wait_ge(chain, links * i + n[0])

                        mean_e, sq_e, mean_o, sq_o = (stats[:, :, k] for k in (1, 2, 4, 5))
                        nc.vector.tensor_tensor(nt["sum"][:], mean_e, mean_o, ALU.add)
                        then(nc.vector.tensor_tensor(nt["gap"][:], mean_e, mean_o, ALU.subtract))
                        then(nc.vector.tensor_tensor(nt["sq"][:], sq_e, sq_o, ALU.add))
                        then(nc.vector.tensor_tensor(nt["gap2"][:], nt["gap"][:], nt["gap"][:], ALU.mult))
                        then(nc.vector.scalar_tensor_tensor(out=nt["sq_all"][:], in0=nt["gap2"][:], scalar=F / 4,
                                                            in1=nt["sq"][:], op0=ALU.mult, op1=ALU.add))
                        nc.vector.tensor_scalar(nt["var"][:], nt["sq_all"][:], 1.0 / F, EPS, ALU.mult,
                                                ALU.add).then_inc(var_made, 1)
                        dve.wait_ge(std_made, i + 1)
                        then(nc.vector.reciprocal(nt["inv"][:], nt["std"][:]))
                        then(nc.vector.tensor_tensor(nt["inv2"][:], nt["inv"][:], nt["inv"][:], ALU.mult))
                        then(nc.vector.tensor_tensor(nt["ratio"][:], nt["inv2"][:], nt["var"][:], ALU.mult))
                        then(nc.vector.tensor_scalar(nt["step"][:], nt["ratio"][:], -0.5, 1.5, ALU.mult, ALU.add))
                        then(nc.vector.tensor_tensor(nt["rstd"][:], nt["inv"][:], nt["step"][:], ALU.mult))
                        nc.vector.scalar_tensor_tensor(out=nt["shift"][:], in0=nt["sum"][:], scalar=-0.5,
                                                       in1=nt["rstd"][:], op0=ALU.mult,
                                                       op1=ALU.mult).then_inc(shift_made, 1)
                        for j in range(NT):
                            dve.wait_ge(h_made, NT * i + j + 1)
                            for s in range(2):
                                dve.wait_ge(dots_done, 2 * NT * i + max(2 * j + s - 1, 0))
                                nc.vector.tensor_tensor_reduce(junk[:, s, :], hs[:, j, 0:F], uv[:, s, :], 1.0, 0.0,
                                                               ALU.mult, ALU.add,
                                                               dots[:, s, j:j + 1]).then_inc(dots_done, 1)
                            if j % GRP == GRP - 1:
                                g = slice(j + 1 - GRP, j + 1)
                                dve.wait_ge(dots_done, 2 * NT * i + 2 * j + 2)
                                nc.vector.tensor_copy(hs[:, g, S], dots[:, 0, g]).then_inc(s_kept, 1)
                        then(nc.vector.tensor_copy(d_all[:, bass.ds(NT * i, NT)], dots[:, 1, :]))
                        assert n[0] == links + 2

        general_path(nc, locals())


def general_path(nc, g):
    x_all, d_all, ae_bc, WT, ident = (g[k] for k in ("x_all", "d_all", "ae_bc", "WT", "ident"))
    table, state, src, dst, edge_attr, out = (g[k] for k in ("table", "state", "src", "dst", "edge_attr", "out"))
    S, WN, CH, NW, NC, F, FE, KF, ROW, ST, N = (g[k] for k in ("S", "WN", "CH", "NW", "NC", "F", "FE", "KF", "ROW", "ST", "N"))
    DEN, MAX, DCOL = F, F + 1, F + 2
    with ExitStack() as ctx:
        def sb(name, shape, dt):
            return ctx.enter_context(nc.sbuf_tensor(name, shape, dt))

        def ps(name, shape):
            return ctx.enter_context(nc.psum_tensor(name, shape, F32))

        def sem(name):
            return ctx.enter_context(nc.semaphore(name))

        first = sb("first", [WN, 10, ST], F32)
        later = sb("later", [CH, CH], F32)
        ones = sb("g_ones", [CH, CH], F32)
        si = sb("si", [CH, 1], I32)
        di = sb("di", [CH, 1], I32)
        ef = sb("g_ef", [CH, FE], F32)
        efj = sb("g_efj", [CH, FE], F32)
        hg = sb("hg", [CH, ROW], F32)
        sg = sb("sg", [CH, ST], F32)
        sn = sb("sn", [CH, ST], F32)
        col = sb("col", [CH, 8], F32)
        arg = sb("arg", [CH, 2], F32)
        ex = sb("g_ex", [CH, 2], F32)
        rep = sb("rep", [CH, 2, CH], F32)
        row = sb("row", [CH, 2, CH], F32)
        eq = sb("eq", [CH, CH], F32)
        m1 = sb("m1", [CH, CH], F32)
        m2 = sb("m2", [CH, CH], F32)
        wt = sb("g_wt", [CH, CH], F32)
        dup = sb("dup", [CH, CH], F32)
        so = sb("so", [CH, 1], I32)
        row_ps = ps("row_ps", [CH, 2, CH])
        sum_ps = ps("sum_ps", [CH, F + 1])
        st = sb("st", [WN, ST], F32)
        rden = sb("g_rden", [WN, 2], F32)
        agg = sb("g_agg", [WN, F], F32)
        aggT = sb("g_aggT", [128, KF, WN], F32)
        ob = sb("g_ob", [WN, F], F32)
        aggT_ps = ps("g_aggT_ps", [128, KF, WN])
        z_ps = ps("g_z_ps", [WN, F])

        made = sem("g_made")
        first_out = sem("g_first_out")
        loaded = sem("g_loaded")
        gathered = sem("g_gathered")
        rows_turned = sem("g_rows_turned")
        rep_made = sem("g_rep_made")
        first_ready = sem("g_first_ready")
        arg_made = sem("g_arg_made")
        ex_made = sem("g_ex_made")
        wt_made = sem("g_wt_made")
        summed = sem("g_summed")
        v = sem("g_v")
        new_state = sem("g_new_state")
        scattered = sem("g_scattered")
        state_in = sem("g_state_in")
        agg_made = sem("g_agg_made")
        agg_turned = sem("g_agg_turned")
        aggT_kept = sem("g_aggT_kept")
        z_made = sem("g_z_made")
        den_made = sem("g_den_made")
        ob_made = sem("g_ob_made")
        pool_at = sem("g_pool_at")
        stored = sem("g_stored")

        chunk_ops = 14
        with nc.Block() as block:
            @block.sync
            def _(sp):
                with sp.Fori(0, 5) as b:
                    sp.wait_ge(first_ready, b + 1)
                    sp.dma_start(state.rearrange("(t p) f -> p t f", p=WN)[:, bass.ds(10 * b, 10), :],
                                 first[:]).then_inc(first_out, 16)
                sp.wait_ge(first_out, 16 * 5)
                with sp.Fori(0, NC) as c:
                    sp.wait_ge(scattered, 16 * c)
                    sp.dma_start(si[:], src[bass.ds(CH * c, CH)].rearrange("(p a) -> p a", a=1)).then_inc(loaded, 16)
                    sp.dma_start(di[:], dst[bass.ds(CH * c, CH)].rearrange("(p a) -> p a", a=1)).then_inc(loaded, 16)
                    sp.dma_start(ef[:], edge_attr[bass.ds(CH * c, CH), :]).then_inc(loaded, 16)
                sp.wait_ge(scattered, 16 * NC)
                with sp.Fori(0, NW) as w:
                    sp.wait_ge(ob_made, w)
                    sp.dma_start(st[:], state[bass.ds(WN * w, WN), :]).then_inc(state_in, 16)
                    sp.wait_ge(ob_made, w + 1)
                    sp.dma_start(out[bass.ds(WN * w, WN), :], ob[:]).then_inc(stored, 16)
                sp.wait_ge(stored, 16 * NW)

            @block.gpsimd
            def _(pool):
                nc.gpsimd.memset(later[:], 1.0).then_inc(made, 1)
                pool.wait_ge(made, 1)
                nc.gpsimd.affine_select(out=later[:], in_=later[:], compare_op=ALU.is_gt, fill=0.0, base=0,
                                        pattern=[[1, CH]], channel_multiplier=-1).then_inc(made, 1)
                pool.wait_ge(first_out, 16 * 5)
                with pool.Fori(0, NC) as c:
                    pool.wait_ge(loaded, 48 * c + 48)
                    pool.sem_inc(pool_at, 1)
                    pool.indirect_dma_start(out=hg[:], **on_row(table, si[:])).then_inc(gathered, 16)
                    pool.indirect_dma_start(out=sg[:], **on_row(state, di[:])).then_inc(gathered, 16)
                    pool.wait_ge(new_state, 4 * c + 4)
                    pool.sem_inc(pool_at, 1)
                    pool.indirect_dma_start(out=state, out_offset=bass.IndirectOffsetOnAxis(ap=so[:], axis=0),
                                            in_=sn[:], in_offset=None, bounds_check=N - 1,
                                            oob_is_err=False).then_inc(scattered, 16)

            @block.tensor
            def _(pe):
                with pe.Fori(0, NC) as c:
                    pe.wait_ge(rep_made, 2 * c + 2)
                    for s in range(2):
                        mm = nc.tensor.transpose(row_ps[:, s, :], rep[:, s, :], ident[0:CH, 0:CH])
                    mm.then_inc(rows_turned, 1)
                    pe.wait_ge(wt_made, c + 1)
                    nc.tensor.matmul(sum_ps[:], wt[:], hg[:, 0:F + 1], start=True, stop=True).then_inc(summed, 1)
                with pe.Fori(0, NW) as w:
                    pe.wait_ge(agg_made, w + 1)
                    for k in range(KF):
                        mm = nc.tensor.transpose(aggT_ps[:, k, :], agg[:, 128 * k:128 * k + 128], ident[0:WN, 0:WN])
                    mm.then_inc(agg_turned, 1)
                    pe.wait_ge(aggT_kept, w + 1)
                    for k in range(KF):
                        mm = nc.tensor.matmul(z_ps[:], aggT[:, k, :], WT[:, k, :], start=(k == 0), stop=(k == KF - 1))
                    mm.then_inc(z_made, 1)

            @block.scalar
            def _(act):
                with act.Fori(0, NC) as c:
                    act.wait_ge(arg_made, 2 * c + 2)
                    nc.scalar.activation(ex[:], arg[:], ACT.Exp).then_inc(ex_made, 1)
                with act.Fori(0, NW) as w:
                    act.wait_ge(agg_turned, w + 1)
                    nc.scalar.copy(aggT[:].rearrange("p k n -> p (k n)"),
                                   aggT_ps[:].rearrange("p k n -> p (k n)")).then_inc(aggT_kept, 1)

            @block.vector
            def _(dve):
                nc.vector.memset(ones[:], 1.0).then_inc(v, 1)
                nc.vector.memset(first[:], 0.0).then_inc(v, 1)
                dve.wait_ge(v, 2)
                nc.vector.memset(first[:, :, MAX], -BIG).then_inc(v, 1)
                dve.wait_ge(v, 3)
                dve.wait_ge(made, 2)
                with dve.Fori(0, 5) as b:
                    dve.wait_ge(first_out, 16 * b)
                    nc.vector.tensor_copy(first[:, :, DCOL], d_all[:, bass.ds(10 * b, 10)]).then_inc(first_ready, 1)
                with dve.Fori(0, NC) as c:
                    n = [3]

                    def then(ins):
                        n[0] += 1
                        ins.then_inc(v, 1)
                        dve.wait_ge(v, chunk_ops * c + n[0])

                    dstf, ee, r, lg, l, mx, m_new, twice = (col[:, i:i + 1] for i in range(8))
                    dve.wait_ge(loaded, 48 * c + 48)
                    dve.wait_ge(gathered, 32 * c + 32)
                    then(nc.vector.tensor_copy(dstf, di[:]))
                    then(nc.vector.tensor_tensor_reduce(efj[:], ef[:], ae_bc[:], 1.0, 0.0, ALU.mult, ALU.add, ee))
                    then(nc.vector.tensor_tensor(r, ee, hg[:, S:S + 1], ALU.add))
                    then(nc.vector.tensor_tensor(lg, r, sg[:, DCOL:DCOL + 1], ALU.add))
                    then(nc.vector.scalar_tensor_tensor(out=l, in0=lg, scalar=SLOPE, in1=lg, op0=ALU.mult,
                                                        op1=ALU.max))
                    nc.vector.tensor_scalar(rep[:, 0, :], ones[:], dstf, None, ALU.mult).then_inc(rep_made, 1)
                    nc.vector.tensor_scalar(rep[:, 1, :], ones[:], l, None, ALU.mult).then_inc(rep_made, 1)
                    dve.wait_ge(rows_turned, c + 1)
                    then(nc.vector.tensor_copy(row[:], row_ps[:]))
                    then(nc.vector.tensor_scalar(eq[:], row[:, 0, :], dstf, None, ALU.is_equal))
                    then(nc.vector.tensor_scalar(m1[:], eq[:], -1.0, BIG, ALU.add, ALU.mult))
                    then(nc.vector.tensor_tensor(m2[:], m1[:], row[:, 1, :], ALU.add))
                    then(nc.vector.tensor_reduce(mx, m2[:], AX.X, ALU.max))
                    then(nc.vector.tensor_tensor(m_new, mx, sg[:, MAX:MAX + 1], ALU.max))
                    nc.vector.tensor_tensor(arg[:, 0:1], l, m_new, ALU.subtract).then_inc(arg_made, 1)
                    nc.vector.tensor_tensor(arg[:, 1:2], sg[:, MAX:MAX + 1], m_new, ALU.subtract).then_inc(arg_made, 1)
                    then(nc.vector.tensor_tensor(dup[:], eq[:], later[:], ALU.mult))
                    then(nc.vector.tensor_reduce(twice, dup[:], AX.X, ALU.max))
                    nc.vector.scalar_tensor_tensor(out=so[:], in0=twice, scalar=float(2 * N), in1=dstf,
                                                   op0=ALU.mult, op1=ALU.add).then_inc(new_state, 1)
                    nc.vector.tensor_copy(sn[:, MAX:MAX + 1], m_new).then_inc(new_state, 1)
                    nc.vector.tensor_copy(sn[:, DCOL:DCOL + 1], sg[:, DCOL:DCOL + 1]).then_inc(new_state, 1)
                    dve.wait_ge(ex_made, c + 1)
                    nc.vector.tensor_scalar(wt[:], eq[:], ex[:, 0:1], None, ALU.mult).then_inc(wt_made, 1)
                    dve.wait_ge(summed, c + 1)
                    then(nc.vector.scalar_tensor_tensor(out=sn[:, 0:F + 1], in0=sg[:, 0:F + 1], scalar=ex[:, 1:2],
                                                        in1=sum_ps[:], op0=ALU.mult, op1=ALU.add))
                    nc.vector.sem_inc(new_state, 1)
                    assert n[0] == chunk_ops + 3
                with dve.Fori(0, NW) as w:
                    dve.wait_ge(state_in, 16 * w + 16)
                    nc.vector.tensor_scalar(rden[:, 0:1], st[:, DEN:DEN + 1], TINY, None,
                                            ALU.max).then_inc(den_made, 1)
                    dve.wait_ge(den_made, 2 * w + 1)
                    nc.vector.reciprocal(rden[:, 1:2], rden[:, 0:1]).then_inc(den_made, 1)
                    dve.wait_ge(den_made, 2 * w + 2)
                    nc.vector.tensor_scalar(agg[:], st[:, 0:F], rden[:, 1:2], None, ALU.mult).then_inc(agg_made, 1)
                    dve.wait_ge(z_made, w + 1)
                    dve.wait_ge(stored, 16 * w)
                    nc.vector.tensor_tensor(ob[:], z_ps[:], x_all[:, bass.ds(w, 1), :].rearrange("p a f -> p (a f)"),
                                            ALU.add).then_inc(ob_made, 1)


def kernel(x, src, dst, edge_attr_64, L0_gnn_W, L0_gnn_A):
    import numpy as np
    import concourse.bacc as bacc
    from concourse.bass_utils import run_bass_kernel_spmd

    nc = bacc.Bacc("TRN2", target_bir_lowering=False, num_devices=1)
    given = {"x": x, "src": src, "dst": dst, "edge_attr": edge_attr_64, "W": L0_gnn_W, "A": L0_gnn_A}
    arrays, aps = {}, {}
    for name, a in given.items():
        a = np.ascontiguousarray(a)
        arrays[f"in_{name}"] = a
        aps[name] = nc.dram_tensor(f"in_{name}", a.shape, mybir.dt.from_np(a.dtype), kind="ExternalInput").ap()
    aps["out"] = nc.dram_tensor("out", tuple(x.shape), F32, kind="ExternalOutput").ap()
    gnn_kernel(nc, **aps)
    return run_bass_kernel_spmd(nc, [arrays], core_ids=[0]).results[0]["out"]
```

```python
from contextlib import ExitStack

import concourse.bass as bass
from concourse import mybir
from concourse.alu_op_type import AluOpType as ALU

ACT = mybir.ActivationFunctionType
F32 = mybir.dt.float32
BF16 = mybir.dt.bfloat16
I32 = mybir.dt.int32
I16 = mybir.dt.int16
AX = mybir.AxisListType

SLOPE = 0.2
EPS = 1e-5
BIG = 2.0 ** 100
TINY = 1e-30
UNROLL = 4
HALO = 64
SHARED = 6
PAD_NODE = 10 ** 6


def on_row(table, index_column):
    return dict(in_=table, in_offset=bass.IndirectOffsetOnAxis(ap=index_column, axis=0), out_offset=None)


class Step:

    def __init__(self, c, i=None):
        self.c, self.i = c, i

    def times(self, m, add=0):
        rest = m * self.c + add
        if self.i is None:
            return rest
        assert rest >= 0, "a wait's value stays above zero"
        return UNROLL * m * self.i + rest

    def turns(self, n, d=0):
        rest = (self.c + d) // n
        return rest if self.i is None else UNROLL // n * self.i + rest

    def plus(self, d):
        return Step(self.c + d, self.i)


def wait(engine, semaphore, value):
    if not isinstance(value, int) or value > 0:
        engine.wait_ge(semaphore, value)


def gnn_kernel(nc, x, src, dst, edge_attr, W, A, out):
    N, F = x.shape
    E, FE = edge_attr.shape
    WN = CH = 125
    NW, NC = N // WN, E // CH
    assert N == NW * WN and E == NC * CH and F == 256
    KF = F // 128
    ONE, S, ROW = F, F + 1, F + 2
    NT, GRP = 10, 5
    NS = NW // NT
    ST = F + 3

    G = NC // NW
    NB = NW + 1
    FRONT = 192
    PADDED = FRONT + CH * (NB * G - 2) + CH + HALO
    BACK = PADDED - FRONT - E
    BACK_ROWS = next(r for r in (16, 15, 14, 13, 12, 11, 10, 9, 8) if BACK % r == 0 and BACK // r + FRONT // 16 <= 256)
    EP = E // CH
    assert FRONT >= CH + HALO
    src_rows = src.rearrange("(b c p) -> c b p", b=10, p=CH)
    dst_rows = dst.rearrange("(b c p) -> c b p", b=10, p=CH)
    RB = NC // 10

    dst_pad = nc.dram_tensor("dst_pad", (PADDED,), I32).ap()
    dst16_pad = nc.dram_tensor("dst16_pad", (NB * G * CH,), I16).ap()
    r_pad = nc.dram_tensor("r_pad", (PADDED,), F32).ap()
    table = nc.dram_tensor("node_table", (N, ROW), F32).ap()
    state = nc.dram_tensor("node_state", (N, ST), F32).ap()

    with ExitStack() as top:
        def sb(name, shape, dt, where=top):
            return where.enter_context(nc.sbuf_tensor(name, shape, dt))

        def ps(name, shape, where=top):
            return where.enter_context(nc.psum_tensor(name, shape, F32))

        def sem(name, where=top):
            return where.enter_context(nc.semaphore(name))

        x_all = sb("x_all", [WN, NW, F], F32)
        d_all = sb("d_all", [WN, NW], F32)
        d3 = sb("d3", [WN, NW + 3, 3], BF16)
        node_id = sb("node_id", [WN, NW + 3], F32)
        iota = sb("iota", [CH, 3 * WN], F32)
        src_all = sb("src_all", [CH, NC], I32)
        rel_all = sb("rel_all", [CH, NB * G], F32)
        flag = sb("flag", [1, 1], I32)
        ae_bc = sb("ae_bc", [WN, FE], F32)
        WT = sb("WT", [128, KF, F], F32)
        ident = sb("ident", [128, 128], F32)

        with ExitStack() as ctx:
            hs = sb("hs", [WN, NT, ROW], F32, ctx)
            w_sb = sb("w_sb", [128, KF, F], F32, ctx)
            a_col = sb("a_col", [128, 2 * KF], F32, ctx)
            a_rep = sb("a_rep", [128, 2 * KF, WN], F32, ctx)
            ones = sb("ones", [128, 128], F32, ctx)
            uv = sb("uv", [WN, 2, F], F32, ctx)
            stats = sb("stats", [WN, NT, 6], F32, ctx)
            nt = {k: sb(f"nt_{k}", [WN, NT], F32, ctx) for k in (
                "sum", "gap", "sq", "gap2", "sq_all", "var", "std", "inv", "inv2", "ratio", "step", "rstd", "shift")}
            dots = sb("dots", [WN, 2, NT], F32, ctx)
            junk = sb("junk", [WN, 2, F], F32, ctx)
            rest = sb("rest", [WN, 2, NW], F32, ctx)
            rows = sb("rows", [RB, 2, 10, CH], I32, ctx)
            rows_f = sb("rows_f", [RB, 2, 10, CH], F32, ctx)
            first_node = sb("first_node", [CH, NB, G], I32, ctx)
            node_i = sb("node_i", [WN, NW + 3], I32, ctx)
            iota_i = sb("iota_i", [CH, 3 * WN], I32, ctx)
            pad_i = sb("pad_i", [16, 256], I32, ctx)
            pad_f = sb("pad_f", [16, 256], F32, ctx)
            pad_16 = sb("pad_16", [G, CH], I16, ctx)
            line = sb("line", [CH, EP + HALO], I32, ctx)
            line_f = sb("line_f", [CH, EP + HALO], F32, ctx)
            line16 = sb("line16", [CH, EP], I16, ctx)
            rise = sb("rise", [CH, 2, EP], F32, ctx)
            low = sb("low", [CH, 6], F32, ctx)
            bad = sb("bad", [CH, 8], F32, ctx)
            bad_row = sb("bad_row", [1, 2], F32, ctx)
            turn_ps = ps("turn_ps", [CH, 4, 512], ctx)
            bad_ps = ps("bad_ps", [1, CH], ctx)
            uv_ps = ps("uv_ps", [WN, 2, F], ctx)
            wt_ps = ps("wt_ps", [128, KF, KF, 128], ctx)

            weights_in = sem("weights_in", ctx)
            x_in = [sem(f"x_in{j}", ctx) for j in range(2)]
            ident_made = sem("ident_made", ctx)
            a_rep_made = sem("a_rep_made", ctx)
            uv_summed = sem("uv_summed", ctx)
            uv_kept = sem("uv_kept", ctx)
            wt_turned = sem("wt_turned", ctx)
            wt_kept = sem("wt_kept", ctx)
            chain = sem("chain", ctx)
            stat_done = sem("stat_done", ctx)
            var_made = sem("var_made", ctx)
            std_made = sem("std_made", ctx)
            shift_made = sem("shift_made", ctx)
            h_made = sem("h_made", ctx)
            dots_done = sem("dots_done", ctx)
            s_kept = sem("s_kept", ctx)
            table_out = [sem(f"table_out{j}", ctx) for j in range(2)]

            rows_in = sem("rows_in", ctx)
            rows_cast = sem("rows_cast", ctx)
            rows_turned = sem("rows_turned", ctx)
            rows_kept = sem("rows_kept", ctx)
            iotas = sem("iotas", ctx)
            pads_made = sem("pads_made", ctx)
            pads_out = sem("pads_out", ctx)
            line_in = sem("line_in", ctx)
            line16_made = sem("line16_made", ctx)
            line16_out = sem("line16_out", ctx)
            rises = sem("rises", ctx)
            lows = sem("lows", ctx)
            bads = sem("bads", ctx)
            bad_turned = sem("bad_turned", ctx)
            split = sem("split", ctx)

            x_tiles = x.rearrange("(t p) f -> p t f", p=WN)
            table_tiles = table.rearrange("(t p) f -> p t f", p=WN)

            with nc.Block() as block:
                @block.sync
                def _(sp):
                    sp.dma_start(w_sb[:], W.rearrange("(c p) i -> p c i", p=128)).then_inc(weights_in, 16)
                    sp.dma_start(a_col[:], A[0, 0:2 * F].rearrange("(c p) -> p c", p=128), allow_slow_non_contiguous=True).then_inc(weights_in, 16)
                    sp.dma_start(ae_bc[:], A[0, 2 * F:2 * F + FE].partition_broadcast(WN)).then_inc(weights_in, 16)
                    sp.dma_start(rows[:, 0], src_rows).then_inc(rows_in, 16)
                    sp.dma_start(rows[:, 1], dst_rows).then_inc(rows_in, 16)
                    line_of = lambda a: a.rearrange("(p k) -> p k", p=CH)
                    back = lambda a: a[FRONT + E:PADDED].rearrange("(p k) -> p k", p=BACK_ROWS)
                    front = lambda a: a[0:FRONT].rearrange("(p k) -> p k", p=16)
                    sp.dma_start(line_of(dst_pad[FRONT:FRONT + E]), line_of(dst)).then_inc(pads_out, 16)
                    sp.wait_ge(pads_made, 4)
                    fc, bc = FRONT // 16, BACK // BACK_ROWS
                    sp.dma_start(front(dst_pad), pad_i[:, 0:fc]).then_inc(pads_out, 16)
                    sp.dma_start(back(dst_pad), pad_i[0:BACK_ROWS, fc:fc + bc]).then_inc(pads_out, 16)
                    sp.dma_start(front(r_pad), pad_f[:, 0:fc]).then_inc(pads_out, 16)
                    sp.dma_start(back(r_pad), pad_f[0:BACK_ROWS, 0:bc]).then_inc(pads_out, 16)
                    sp.dma_start(dst16_pad[0:CH].rearrange("(p k) -> p k", p=1), pad_16[0:1, :]).then_inc(pads_out, 16)
                    sp.dma_start(dst16_pad[CH + E:].rearrange("(p k) -> p k", k=CH), pad_16[1:G, :]).then_inc(pads_out, 16)
                    sp.wait_ge(pads_out, 16 * 7)
                    sp.dma_start(line[:], bass.AP(tensor=dst_pad.tensor, offset=FRONT,
                                                  ap=[[EP, CH], [1, EP + HALO]])).then_inc(line_in, 16)
                    sp.wait_ge(line16_made, 1)
                    sp.dma_start(line_of(dst16_pad[CH:CH + E]), line16[:]).then_inc(line16_out, 16)
                    sp.wait_ge(line16_out, 16)

                @block.gpsimd
                def _(pool):
                    with pool.Fori(0, NS) as i:
                        for j in range(2):
                            pool.wait_ge(x_in[j], 16 * i)
                            t = bass.ds(NT * i + GRP * j, GRP)
                            pool.dma_start(x_all[:, t, :], x_tiles[:, t, :]).then_inc(x_in[j], 16)
                    nc.gpsimd.memset(pad_i[:], PAD_NODE).then_inc(iotas, 1)
                    nc.gpsimd.memset(pad_f[:], 0.0).then_inc(pads_made, 1)
                    nc.gpsimd.memset(pad_16[:], -1).then_inc(pads_made, 1)
                    pool.wait_ge(iotas, 1)
                    nc.gpsimd.memset(pad_i[:, 0:FRONT // 16], -PAD_NODE).then_inc(pads_made, 2)
                    nc.gpsimd.memset(ident[:], 0.0).then_inc(ident_made, 1)
                    pool.wait_ge(ident_made, 1)
                    nc.gpsimd.affine_select(out=ident[:], in_=ident[:], compare_op=ALU.not_equal, fill=1.0, base=0,
                                            pattern=[[-1, 128]], channel_multiplier=1).then_inc(ident_made, 1)
                    nc.gpsimd.iota(first_node[:], pattern=[[WN, NB], [0, G]], base=0,
                                   channel_multiplier=0).then_inc(iotas, 1)
                    nc.gpsimd.iota(node_i[:], pattern=[[WN, NW + 3]], base=-WN, channel_multiplier=1).then_inc(iotas, 1)
                    nc.gpsimd.iota(iota_i[:], pattern=[[1, 3 * WN]], base=-WN, channel_multiplier=0).then_inc(iotas, 1)
                    pool.wait_ge(iotas, 4)
                    nc.gpsimd.tensor_copy(node_id[:], node_i[:]).then_inc(iotas, 1)
                    nc.gpsimd.tensor_copy(iota[:], iota_i[:]).then_inc(iotas, 1)
                    pool.wait_ge(line16_made, 2)
                    nc.gpsimd.tensor_tensor(rise[:, 0], line_f[:, 1:EP + 1], line_f[:, 0:EP], ALU.subtract).then_inc(rises, 1)
                    nc.gpsimd.tensor_tensor(rise[:, 1], line_f[:, HALO:EP + HALO], line_f[:, 0:EP],
                                            ALU.subtract).then_inc(rises, 1)
                    with pool.Fori(0, NS) as i:
                        for j in range(2):
                            pool.wait_ge(s_kept, 2 * i + j + 1)
                            pool.dma_start(table_tiles[:, bass.ds(NT * i + GRP * j, GRP), :],
                                           hs[:, GRP * j:GRP * j + GRP, :]).then_inc(table_out[j], 16)
                    for j in range(2):
                        pool.wait_ge(table_out[j], 16 * NS)

                @block.tensor
                def _(pe):
                    pe.wait_ge(ident_made, 2)
                    pe.wait_ge(weights_in, 48)
                    for a in range(KF):
                        for b in range(KF):
                            mm = nc.tensor.transpose(wt_ps[:, a, b, :], w_sb[:, b, 128 * a:128 * a + 128], ident[:])
                    mm.then_inc(wt_turned, 1)
                    pe.wait_ge(a_rep_made, 2 * KF)
                    for s in range(2):
                        for c in range(KF):
                            mm = nc.tensor.matmul(uv_ps[:, s, :], a_rep[:, KF * s + c, :], w_sb[:, c, :],
                                                  start=(c == 0), stop=(c == KF - 1))
                    mm.then_inc(uv_summed, 1)
                    for q in range(4):
                        pe.wait_ge(rows_cast, q // 2 + 1)
                        for b in range(5):
                            mm = nc.tensor.transpose(turn_ps[:, q, RB * b:RB * b + RB],
                                                     rows_f[:, q // 2, 5 * (q % 2) + b, :], ident[0:RB, 0:RB])
                        mm.then_inc(rows_turned, 1)
                    pe.wait_ge(bads, 3)
                    nc.tensor.transpose(bad_ps[:], bad[:, 6:7], ident[0:CH, 0:CH]).then_inc(bad_turned, 1)

                @block.scalar
                def _(act):
                    act.wait_ge(rows_in, 32)
                    for s in range(2):
                        nc.scalar.copy(rows_f[:, s], rows[:, s]).then_inc(rows_cast, 1)
                    act.wait_ge(wt_turned, 1)
                    nc.scalar.copy(WT[:].rearrange("p a f -> p (a f)"),
                                   wt_ps[:].rearrange("p a b f -> p (a b f)")).then_inc(wt_kept, 1)
                    for q in range(2):
                        act.wait_ge(rows_turned, q + 1)
                        nc.scalar.copy(src_all[:, 5 * RB * q:5 * RB * (q + 1)], turn_ps[:, q, 0:5 * RB]).then_inc(wt_kept, 1)
                    act.wait_ge(line_in, 16)
                    nc.scalar.copy(line16[:], line[:, 0:EP]).then_inc(line16_made, 1)
                    nc.scalar.copy(line_f[:], line[:]).then_inc(line16_made, 1)
                    with act.Fori(0, NS) as i:
                        act.wait_ge(var_made, i + 1)
                        nc.scalar.activation(nt["std"][:], nt["var"][:], ACT.Sqrt).then_inc(std_made, 1)
                        act.wait_ge(shift_made, i + 1)
                        for j in range(NT):
                            if j % GRP == 0:
                                act.wait_ge(table_out[j // GRP], 16 * i)
                            nc.scalar.activation(hs[:, j, 0:F], x_all[:, bass.ds(NT * i + j, 1), :], ACT.Relu,
                                                 bias=nt["shift"][:, j:j + 1],
                                                 scale=nt["rstd"][:, j:j + 1]).then_inc(h_made, 1)

                @block.vector
                def _(dve):
                    nc.vector.memset(ones[:], 1.0).then_inc(chain, 1)
                    nc.vector.memset(hs[:, :, ONE], 1.0).then_inc(chain, 1)
                    dve.wait_ge(chain, 2)
                    dve.wait_ge(weights_in, 48)
                    for c in range(2 * KF):
                        nc.vector.tensor_scalar(a_rep[:, c, :], ones[:, 0:WN], a_col[:, c:c + 1], None,
                                                ALU.mult).then_inc(a_rep_made, 1)
                    dve.wait_ge(uv_summed, 1)
                    nc.vector.tensor_copy(uv[:], uv_ps[:]).then_inc(uv_kept, 1)
                    dve.wait_ge(uv_kept, 1)
                    nc.vector.memset(d3[:], 0.0).then_inc(split, 1)
                    nc.vector.memset(rel_all[:], -float(PAD_NODE)).then_inc(rows_kept, 1)
                    dve.wait_ge(rows_kept, 1)
                    dve.wait_ge(iotas, 2)
                    base = first_node[:].rearrange("p k g -> p (k g)")
                    for q in range(2):
                        dve.wait_ge(rows_turned, 3 + q)
                        cols = slice(1 + 5 * RB * q, 1 + 5 * RB * (q + 1))
                        nc.vector.tensor_tensor(rel_all[:, cols], turn_ps[:, 2 + q, 0:5 * RB], base[:, cols],
                                                ALU.subtract).then_inc(rows_kept, 1)
                    dve.wait_ge(rows_kept, 3)
                    dve.wait_ge(rises, 2)
                    rel = rel_all[:].rearrange("p (k g) -> p k g", g=G)
                    for n, (what, op) in enumerate((
                            (rel[:, 1:NB, 0], ALU.min), (rel[:, 0:NW, SHARED + 1], ALU.min),
                            (rel[:, 0:NW, G - SHARED], ALU.max), (rel[:, 0:NW, G - 1], ALU.max),
                            (rise[:, 0], ALU.min), (rise[:, 1], ALU.min))):
                        nc.vector.tensor_reduce(low[:, n:n + 1], what, AX.X, op).then_inc(lows, 1)
                    dve.wait_ge(lows, 6)
                    for n, (m, a) in enumerate(((-1, -WN), (-1, 0), (1, 1 - WN), (1, 1 - 2 * WN), (-1, 0), (-1, 1))):
                        nc.vector.tensor_scalar(bad[:, n:n + 1], low[:, n:n + 1], float(m), float(a), ALU.mult,
                                                ALU.add).then_inc(lows, 1)
                    dve.wait_ge(lows, 12)
                    nc.vector.tensor_reduce(bad[:, 6:7], bad[:, 0:6], AX.X, ALU.max).then_inc(bads, 3)
                    dve.wait_ge(bad_turned, 1)
                    nc.vector.tensor_reduce(bad_row[:, 0:1], bad_ps[:], AX.X, ALU.max).then_inc(bads, 1)
                    dve.wait_ge(bads, 4)
                    nc.vector.tensor_scalar(flag[:], bad_row[:, 0:1], 0.0, None, ALU.is_gt).then_inc(bads, 1)
                    links = 10
                    with dve.Fori(0, NS) as i:
                        for j in range(NT):
                            if j % GRP == 0:
                                dve.wait_ge(x_in[j // GRP], 16 * i + 16)
                            nc.vector.bn_stats(stats[:, j, :], x_all[:, bass.ds(NT * i + j, 1), :]
                                               .rearrange("p a f -> p (a f)")).then_inc(stat_done, 1)
                        dve.wait_ge(stat_done, NT * i + NT)
                        n = [2]

                        def then(ins):
                            n[0] += 1
                            ins.then_inc(chain, 1)
                            dve.wait_ge(chain, links * i + n[0])

                        mean_e, sq_e, mean_o, sq_o = (stats[:, :, k] for k in (1, 2, 4, 5))
                        nc.vector.tensor_tensor(nt["sum"][:], mean_e, mean_o, ALU.add)
                        then(nc.vector.tensor_tensor(nt["gap"][:], mean_e, mean_o, ALU.subtract))
                        then(nc.vector.tensor_tensor(nt["sq"][:], sq_e, sq_o, ALU.add))
                        then(nc.vector.tensor_tensor(nt["gap2"][:], nt["gap"][:], nt["gap"][:], ALU.mult))
                        then(nc.vector.scalar_tensor_tensor(out=nt["sq_all"][:], in0=nt["gap2"][:], scalar=F / 4,
                                                            in1=nt["sq"][:], op0=ALU.mult, op1=ALU.add))
                        nc.vector.tensor_scalar(nt["var"][:], nt["sq_all"][:], 1.0 / F, EPS, ALU.mult,
                                                ALU.add).then_inc(var_made, 1)
                        dve.wait_ge(std_made, i + 1)
                        then(nc.vector.reciprocal(nt["inv"][:], nt["std"][:]))
                        then(nc.vector.tensor_tensor(nt["inv2"][:], nt["inv"][:], nt["inv"][:], ALU.mult))
                        then(nc.vector.tensor_tensor(nt["ratio"][:], nt["inv2"][:], nt["var"][:], ALU.mult))
                        then(nc.vector.tensor_scalar(nt["step"][:], nt["ratio"][:], -0.5, 1.5, ALU.mult, ALU.add))
                        then(nc.vector.tensor_tensor(nt["rstd"][:], nt["inv"][:], nt["step"][:], ALU.mult))
                        nc.vector.scalar_tensor_tensor(out=nt["shift"][:], in0=nt["sum"][:], scalar=-0.5,
                                                       in1=nt["rstd"][:], op0=ALU.mult,
                                                       op1=ALU.mult).then_inc(shift_made, 1)
                        for j in range(NT):
                            dve.wait_ge(h_made, NT * i + j + 1)
                            for s in range(2):
                                dve.wait_ge(dots_done, 2 * NT * i + max(2 * j + s - 1, 0))
                                nc.vector.tensor_tensor_reduce(junk[:, s, :], hs[:, j, 0:F], uv[:, s, :], 1.0, 0.0,
                                                               ALU.mult, ALU.add,
                                                               dots[:, s, j:j + 1]).then_inc(dots_done, 1)
                            if j % GRP == GRP - 1:
                                g = slice(j + 1 - GRP, j + 1)
                                dve.wait_ge(dots_done, 2 * NT * i + 2 * j + 2)
                                nc.vector.tensor_copy(hs[:, g, S], dots[:, 0, g]).then_inc(s_kept, 1)
                        then(nc.vector.tensor_copy(d_all[:, bass.ds(NT * i, NT)], dots[:, 1, :]))
                        assert n[0] == links + 2
                    high, mid, low_part = (d3[:, 1:NW + 1, k] for k in range(3))
                    for n, ins in enumerate((
                            lambda: nc.vector.tensor_copy(high, d_all[:]),
                            lambda: nc.vector.tensor_tensor(rest[:, 0], d_all[:], high, ALU.subtract),
                            lambda: nc.vector.tensor_copy(mid, rest[:, 0]),
                            lambda: nc.vector.tensor_tensor(rest[:, 1], rest[:, 0], mid, ALU.subtract),
                            lambda: nc.vector.tensor_copy(low_part, rest[:, 1]))):
                        dve.wait_ge(split, n + 1)
                        ins().then_inc(split, 1)

        shared = dict(locals())
        sorted_path(nc, shared)
        general_path(nc, shared)


def sorted_path(nc, g):
    x_all, d3, node_id, iota, ae_bc, WT, ident = (g[k] for k in (
        "x_all", "d3", "node_id", "iota", "ae_bc", "WT", "ident"))
    src_all, rel_all, flag = (g[k] for k in ("src_all", "rel_all", "flag"))
    table, dst_pad, dst16_pad, r_pad = (g[k] for k in ("table", "dst_pad", "dst16_pad", "r_pad"))
    edge_attr, out = (g[k] for k in ("edge_attr", "out"))
    WN, CH, NW, NC, NB, G, F, FE, KF, ROW, S, FRONT = (g[k] for k in (
        "WN", "CH", "NW", "NC", "NB", "G", "F", "FE", "KF", "ROW", "S", "FRONT"))
    GE = G * CH
    WIDE = CH + 2 * HALO
    LEFT, RIGHT = SHARED + 1, SHARED - 1
    FRONT_P = 112

    chunk_list = ([(-1, G - RIGHT + b) for b in range(RIGHT)] + [(0, b) for b in range(G)]
                  + [(1, b) for b in range(LEFT)])
    PER_WINDOW = len(chunk_list)
    parts = [range(0, 6), range(6, 12), range(12, 17), range(17, 22), range(22, PER_WINDOW)]
    EARLY = 4
    assert RIGHT + G == 22

    def in_window(w, n):
        kb, b = chunk_list[n]
        if w.i is not None:
            return True
        return 0 <= G * (w.c + kb) - 1 + b < NC

    with ExitStack() as ctx:
        def sb(name, shape, dt):
            return ctx.enter_context(nc.sbuf_tensor(name, shape, dt))

        def ps(name, shape):
            return ctx.enter_context(nc.psum_tensor(name, shape, F32))

        def sem(name):
            return ctx.enter_context(nc.semaphore(name))

        rows = sb("gathered_rows", [CH, UNROLL, G, ROW], F32)
        index = sb("index", [CH, UNROLL, G], I32)
        ef = sb("ef", [CH, 2, G, FE], F32)
        ef_a = sb("ef_a", [CH, G, FE], F32)
        ee = sb("ee", [CH, 2, G], F32)
        r = sb("r", [CH, 2, G], F32)
        r_row = sb("r_row", [G, 2, CH], F32)
        dst_bc = sb("dst_bc", [128, 2, GE], I16)
        is_dst = sb("is_dst", [WN, GE + (LEFT + RIGHT) * CH], BF16)
        d3_now = sb("d3_now", [WN, 2, 3, 3], BF16)
        d_dst = sb("d_dst", [CH, G], F32)
        dst_wide = sb("dst_wide", [G, 2, WIDE], I32)
        fall = sb("fall", [G, WIDE - 1], F32)
        cut = sb("cut", [G, 2, WIDE - 1], F32)
        r_wide = sb("r_wide", [G, 2, WIDE], F32)
        fwd = sb("fwd", [G, WIDE], F32)
        bwd = sb("bwd", [G, WIDE], F32)
        top = sb("top", [G, CH], F32)
        both = sb("both", [CH, 2, G], F32)
        leaky = sb("leaky", [CH, 2, G], F32)
        below = sb("below", [CH, G], F32)
        ex = sb("ex", [CH, 2, G], F32)
        rel = sb("rel", [CH, 2, G], F32)
        wts = sb("wts", [CH, PER_WINDOW, WN], F32)
        den = sb("den", [WN, 2], F32)
        agg = sb("agg", [WN, F], F32)
        aggT = sb("aggT", [128, KF, WN], F32)
        o = sb("o", [WN, 2, F], F32)
        acc = ps("acc", [WN, 2, 512])
        z_ps = ps("z_ps", [WN, F])
        aggT_ps = ps("aggT_ps", [128, KF, WN])
        d_ps = ps("d_ps", [CH, 2, 512])
        r_ps = ps("r_ps", [G, CH])
        both_ps = ps("both_ps", [CH, 2, G])

        loaded = [sem(f"loaded{h}") for h in range(2)]
        prepared = sem("prepared")
        index_made = sem("index_made")
        gathered = [sem(f"gathered{s}") for s in range(UNROLL)]
        slot_free = sem("slot_free")
        ef_a_made = sem("ef_a_made")
        ee_made = sem("ee_made")
        r_made = sem("r_made")
        r_turned = sem("r_turned")
        r_row_made = sem("r_row_made")
        r_out = [sem(f"r_out{h}") for h in range(2)]
        r_wide_in = [sem(f"r_wide_in{h}") for h in range(2)]
        is_dst_made = sem("is_dst_made")
        d_summed = sem("d_summed")
        d_kept = sem("d_kept")
        fall_made = sem("fall_made")
        scanned = sem("scanned")
        top_made = sem("top_made")
        both_turned = sem("both_turned")
        both_made = sem("both_made")
        leaky_made = sem("leaky_made")
        below_made = sem("below_made")
        ex_made = sem("ex_made")
        rel_kept = sem("rel_kept")
        wts_made = sem("wts_made")
        wts_used = sem("wts_used")
        den_made = sem("den_made")
        agg_made = sem("agg_made")
        agg_turned = sem("agg_turned")
        aggT_kept = sem("aggT_kept")
        z_made = sem("z_made")
        o_made = sem("o_made")
        stored = [sem(f"stored{h}") for h in range(2)]
        pool_at = sem("pool_at")
        pe_at = sem("pe_at")

        def steps(engine, one):
            one(Step(0))
            one(Step(1))
            turns = (NW - 4) // UNROLL
            with engine.Fori(0, turns) as i:
                for c in range(UNROLL):
                    one(Step(2 + c, i))
            for c in range(2 + UNROLL * turns, NW + 2):
                one(Step(c))

        def has(k, d, n):
            return k.i is not None or 0 <= k.c + d < n

        def if_sorted(engine, body):
            bad = engine.value_load(flag[0:1, 0:1], min_val=0, max_val=1)
            with engine.If(bad == 0):
                body()
            with engine.Else():
                engine.nop()

        with nc.Block() as block:
            @block.sync
            def _(sp):
                def load(k):
                    h = k.c % 2
                    edges = k.times(GE)
                    wait(sp, prepared, k.times(1, -1))
                    if has(k, 0, NW):
                        for p, n in ((0, FRONT_P), (FRONT_P, CH - FRONT_P)):
                            sp.dma_start(ef[p:p + n, h], edge_attr[bass.ds(edges, GE), :].rearrange(
                                "(g p) c -> p g c", p=CH)[p:p + n]).then_inc(loaded[h], 16)
                    sp.dma_start(dst_bc[:, h], dst16_pad[bass.ds(edges, GE)].partition_broadcast(128)
                                 ).then_inc(loaded[h], 16)
                    sp.dma_start(dst_wide[:, h], wide_rows(dst_pad, k)).then_inc(loaded[h], 16)

                def wide_rows(padded, k):
                    at = padded[bass.ds(k.times(GE, FRONT - CH - HALO), (G - 1) * CH + WIDE)]
                    return bass.AP(tensor=at.tensor, offset=at.offset, ap=[[CH, G], [1, WIDE]])

                def one(k):
                    h = k.c % 2
                    if has(k, 2, NB):
                        load(k.plus(2))
                    if has(k, 0, NB):
                        wait(sp, both_turned, k.times(1, -1))
                        wait(sp, r_out[h], 16 * k.turns(2, 2) if has(k, 0, NW) else 0)
                        if not has(k, 0, NW):
                            sp.wait_ge(r_out[1 - h], 16 * k.turns(2, 1))
                        sp.dma_start(r_wide[:, h], wide_rows(r_pad, k)).then_inc(r_wide_in[h], 16)
                    if has(k, -2, NW):
                        w = k.plus(-2)
                        wait(sp, o_made, k.times(1, -1))
                        for p, n in ((0, FRONT_P), (FRONT_P, WN - FRONT_P)):
                            sp.dma_start(out[bass.ds(w.times(WN, p), n), :], o[p:p + n, h]).then_inc(stored[h], 16)

                def body():
                    load(Step(0))
                    load(Step(1))
                    steps(sp, one)
                    sp.wait_ge(stored[0], 32 * ((NW + 1) // 2))
                    sp.wait_ge(stored[1], 32 * (NW // 2))

                if_sorted(sp, body)

            @block.gpsimd
            def _(pool):
                def one(k):
                    s = k.c % UNROLL
                    if not has(k, 0, NW):
                        return
                    wait(pool, slot_free, k.times(1, 1))
                    wait(pool, index_made, k.times(1, 1))
                    pool.sem_inc(pool_at, 1)
                    for j in range(G):
                        pool.indirect_dma_start(out=rows[:, s, j, :],
                                                **on_row(table, index[:, s, j:j + 1])).then_inc(gathered[s], 16)

                def body():
                    pool.sem_inc(slot_free, UNROLL)
                    steps(pool, one)

                if_sorted(pool, body)

            @block.tensor
            def _(pe):
                def targets(k):
                    h = k.c % 2
                    wait(pe, is_dst_made, k.times(1, 1))
                    wait(pe, d_kept, k.times(1, -1))
                    for b in range(G):
                        hot = [(is_dst[:, CH * b:CH * b + CH], 1)]
                        if b < LEFT:
                            hot.append((is_dst[:, GE + CH * b:GE + CH * b + CH], 0))
                        if b >= G - RIGHT:
                            at = GE + CH * (LEFT + b - (G - RIGHT))
                            hot.append((is_dst[:, at:at + CH], 2))
                        for n, (one_hot, w) in enumerate(hot):
                            mm = nc.tensor.matmul(d_ps[:, h, 3 * b:3 * b + 3], one_hot, d3_now[:, h, w, :],
                                                  start=(n == 0), stop=(n == len(hot) - 1))
                    mm.then_inc(d_summed, 1)

                def sums(w, part):
                    mine = [n for n in parts[part] if in_window(w, n)]
                    if mine:
                        wait(pe, wts_made, w.times(5, part))
                    first = next(n for n in range(PER_WINDOW) if in_window(w, n))
                    last = max(n for n in range(PER_WINDOW) if in_window(w, n))
                    for n in mine:
                        kb, b = chunk_list[n]
                        chunk = G * (w.c + kb) - 1 + b
                        mm = nc.tensor.matmul(acc[:, w.c % 2, 0:F + 1], wts[:, n, :],
                                              rows[:, chunk // G % UNROLL, chunk % G, 0:F + 1],
                                              start=(n == first), stop=(n == last))
                    if mine:
                        mm.then_inc(wts_used, 1)
                    if part == 0 and mine:
                        pe.wait_ge(wts_used, w.times(5, 0))
                        pe.sem_inc(slot_free, 1)

                def one(k):
                    w, z = k.plus(-1), k.plus(-2)
                    if has(k, 0, NW):
                        wait(pe, r_made, k.times(1, 1))
                        wait(pe, r_row_made, k.times(1))
                        nc.tensor.transpose(r_ps[:], r[:, k.c % 2, :], ident[0:CH, 0:CH]).then_inc(r_turned, 1)
                    if has(k, 1, NB):
                        targets(k.plus(1))
                    if has(k, -1, NW):
                        wait(pe, agg_made, k.times(1, -2))
                        sums(w, 0)
                        sums(w, 1)
                    if has(k, 0, NB):
                        wait(pe, top_made, k.times(1, 1))
                        wait(pe, both_made, k.times(1))
                        pe.sem_inc(pe_at, 1)
                        nc.tensor.transpose(both_ps[:, 0, :], r_wide[:, k.c % 2, HALO:HALO + CH], ident[0:G, 0:G])
                        nc.tensor.transpose(both_ps[:, 1, :], top[:], ident[0:G, 0:G]).then_inc(both_turned, 1)
                    if has(k, -2, NW):
                        wait(pe, agg_made, k.times(1, -1))
                        wait(pe, aggT_kept, k.times(1, -2))
                        for c in range(KF):
                            mm = nc.tensor.transpose(aggT_ps[:, c, :], agg[:, 128 * c:128 * c + 128],
                                                     ident[0:WN, 0:WN])
                        mm.then_inc(agg_turned, 1)
                    if has(k, -1, NW):
                        sums(w, 2)
                        sums(w, 3)
                    if has(k, -2, NW):
                        wait(pe, aggT_kept, k.times(1, -1))
                        wait(pe, o_made, k.times(1, -2))
                        for c in range(KF):
                            mm = nc.tensor.matmul(z_ps[:], aggT[:, c, :], WT[:, c, :], start=(c == 0),
                                                  stop=(c == KF - 1))
                        mm.then_inc(z_made, 1)
                    if has(k, -1, NW):
                        sums(w, 4)

                def body():
                    targets(Step(0))
                    steps(pe, one)

                if_sorted(pe, body)

            @block.scalar
            def _(act):
                def indices(k):
                    nc.scalar.copy(index[:, k.c % UNROLL, :], src_all[:, bass.ds(k.times(G), G)]).then_inc(index_made, 1)

                def one(k):
                    h = k.c % 2
                    if has(k, 2, NW):
                        indices(k.plus(2))
                    if has(k, 0, NW):
                        wait(act, r_turned, k.times(1, 1))
                        wait(act, r_out[h], 16 * k.turns(2))
                        nc.scalar.copy(r_row[:, h, :], r_ps[:]).then_inc(r_row_made, 1)
                        wait(act, r_row_made, k.times(1, 1))
                        act.dma_start(r_pad[bass.ds(k.times(GE, FRONT), GE)].rearrange("(g p) -> g p", p=CH),
                                      r_row[:, h, :]).then_inc(r_out[h], 16)
                    if has(k, -2, NW):
                        wait(act, den_made, k.times(2, -2))
                        wait(act, agg_turned, k.times(1, -2))
                        nc.scalar.mul(agg[:], acc[:, h, 0:F], den[:, 1:2]).then_inc(agg_made, 1)
                        wait(act, agg_turned, k.times(1, -1))
                        wait(act, z_made, k.times(1, -2))
                        nc.scalar.copy(aggT[:].rearrange("p k n -> p (k n)"),
                                       aggT_ps[:].rearrange("p k n -> p (k n)")).then_inc(aggT_kept, 1)
                    if has(k, 0, NB):
                        wait(act, below_made, k.times(1, 1))
                        nc.scalar.activation(ex[:, h, :], below[:], ACT.Exp).then_inc(ex_made, 1)

                def body():
                    indices(Step(0))
                    indices(Step(1))
                    steps(act, one)

                if_sorted(act, body)

            @block.vector
            def _(dve):
                def prepare(k):
                    h = k.c % 2
                    n_loads = 4
                    if has(k, 0, NW):
                        dve.wait_ge(loaded[h], 16 * n_loads * k.turns(2, 2) if k.i is None
                                    else 16 * n_loads * k.turns(2, 2))
                    else:
                        dve.wait_ge(loaded[h], 16 * (n_loads * k.turns(2) + 2))
                    wait(dve, d_summed, k.times(1))
                    for to, of, w in ((slice(0, GE), slice(0, GE), 1),
                                      (slice(GE, GE + LEFT * CH), slice(0, LEFT * CH), 0),
                                      (slice(GE + LEFT * CH, None), slice(GE - RIGHT * CH, GE), 2)):
                        nc.vector.tensor_scalar(is_dst[:, to], dst_bc[0:WN, h, of],
                                                node_id[:, bass.ds(k.times(1, w), 1)], None, ALU.is_equal)
                    nc.vector.tensor_copy(d3_now[:, h], d3[:, bass.ds(k.times(1), 3), :]).then_inc(is_dst_made, 1)
                    wait(dve, fall_made, k.times(2))
                    nc.vector.tensor_tensor(fall[:], dst_wide[:, h, 0:WIDE - 1], dst_wide[:, h, 1:WIDE],
                                            ALU.subtract).then_inc(fall_made, 1)
                    if has(k, 0, NW):
                        nc.vector.tensor_tensor(ef_a[:], ef[:, h], ae_bc[:].unsqueeze(1).broadcast_to([CH, G, FE]),
                                                ALU.mult).then_inc(ef_a_made, 1)
                    dve.wait_ge(fall_made, k.times(2, 1))
                    nc.vector.tensor_scalar(cut[:, h, :], fall[:], BIG, None, ALU.mult).then_inc(fall_made, 1)
                    if has(k, 0, NW):
                        dve.wait_ge(ef_a_made, k.times(1, 1))
                        nc.vector.tensor_reduce(ee[:, h, :], ef_a[:], AX.X, ALU.add).then_inc(ee_made, 1)
                    dve.wait_ge(fall_made, k.times(2, 2))
                    dve.sem_inc(prepared, 1)

                def weights(w, part):
                    mine = [n for n in parts[part] if in_window(w, n)]
                    if not mine:
                        return
                    wait(dve, wts_used, w.times(5, part - 5) if w.i is not None or w.c else 0)
                    for n in mine:
                        kb, b = chunk_list[n]
                        h = (w.c + kb) % 2
                        at = WN * (1 - kb)
                        ins = nc.vector.tensor_scalar(wts[:, n, :], iota[:, at:at + WN], rel[:, h, b:b + 1],
                                                      ex[:, h, b:b + 1], ALU.is_equal, ALU.mult)
                    ins.then_inc(wts_made, 1)

                def one(k):
                    h = k.c % 2
                    if has(k, 0, NW):
                        s = k.c % UNROLL
                        dve.wait_ge(gathered[s], 16 * G * k.turns(UNROLL, UNROLL))
                        dve.wait_ge(ee_made, k.times(1, 1))
                        nc.vector.tensor_tensor(r[:, h, :], rows[:, s, :, S], ee[:, h, :], ALU.add).then_inc(r_made, 1)
                    if has(k, -2, NW):
                        dve.wait_ge(wts_used, k.times(5, -6))
                        nc.vector.tensor_scalar(den[:, 0:1], acc[:, h, F:F + 1], TINY, None, ALU.max).then_inc(den_made, 1)
                        dve.wait_ge(den_made, k.times(2, -3))
                        nc.vector.reciprocal(den[:, 1:2], den[:, 0:1]).then_inc(den_made, 1)
                    if has(k, 1, NB):
                        prepare(k.plus(1))
                    if has(k, 0, NB):
                        dve.wait_ge(d_summed, k.times(1, 1))
                        nc.vector.tensor_reduce(d_dst[:], d_ps[:, h, 0:3 * G].rearrange("p (g c) -> p g c", c=3), AX.X, ALU.add).then_inc(d_kept, 1)
                        wait(dve, wts_made, k.times(5, -2))
                        nc.vector.tensor_copy(rel[:, h, :], rel_all[:, bass.ds(k.times(G), G)]).then_inc(rel_kept, 1)
                        dve.wait_ge(r_wide_in[h], 16 * k.turns(2, 2))
                        nc.vector.tensor_tensor_scan(fwd[:, 1:HALO + CH], cut[:, h, 0:HALO + CH - 1],
                                                     r_wide[:, h, 1:HALO + CH], -BIG, ALU.add, ALU.max)
                        nc.vector.tensor_tensor_scan(bwd[:, WIDE - 2:HALO - 1:-1], cut[:, h, WIDE - 2:HALO - 1:-1],
                                                     r_wide[:, h, WIDE - 2:HALO - 1:-1], -BIG, ALU.add,
                                                     ALU.max).then_inc(scanned, 1)
                        dve.wait_ge(scanned, k.times(1, 1))
                        nc.vector.tensor_tensor(top[:], fwd[:, HALO:HALO + CH], bwd[:, HALO:HALO + CH],
                                                ALU.max).then_inc(top_made, 1)
                        dve.wait_ge(both_turned, k.times(1, 1))
                        dve.wait_ge(d_kept, k.times(1, 1))
                        nc.vector.tensor_tensor(both[:], both_ps[:], d_dst[:].unsqueeze(1).broadcast_to([CH, 2, G]),
                                                ALU.add).then_inc(both_made, 1)
                        dve.wait_ge(both_made, k.times(1, 1))
                        nc.vector.scalar_tensor_tensor(out=leaky[:], in0=both[:], scalar=SLOPE, in1=both[:],
                                                       op0=ALU.mult, op1=ALU.max).then_inc(leaky_made, 1)
                        dve.wait_ge(leaky_made, k.times(1, 1))
                        nc.vector.tensor_tensor(below[:], leaky[:, 0], leaky[:, 1], ALU.subtract).then_inc(below_made, 1)
                        dve.wait_ge(ex_made, k.times(1, 1))
                        dve.wait_ge(rel_kept, k.times(1, 1))
                    if has(k, -1, NW):
                        weights(k.plus(-1), EARLY)
                    if has(k, 0, NW):
                        for part in range(EARLY):
                            weights(k, part)
                    if has(k, -2, NW):
                        dve.wait_ge(z_made, k.times(1, -1))
                        wait(dve, stored[h], 32 * k.turns(2, -2))
                        nc.vector.tensor_tensor(o[:, h, :], z_ps[:], x_all[:, bass.ds(k.times(1, -2), 1), :]
                                                .rearrange("p a f -> p (a f)"), ALU.add).then_inc(o_made, 1)

                def body():
                    prepare(Step(0))
                    steps(dve, one)

                if_sorted(dve, body)


def general_path(nc, g):
    x_all, d_all, ae_bc, WT, ident, flag = (g[k] for k in ("x_all", "d_all", "ae_bc", "WT", "ident", "flag"))
    table, state, src, dst, edge_attr, out = (g[k] for k in ("table", "state", "src", "dst", "edge_attr", "out"))
    S, WN, CH, NW, NC, F, FE, KF, ROW, ST, N = (g[k] for k in ("S", "WN", "CH", "NW", "NC", "F", "FE", "KF", "ROW", "ST", "N"))
    DEN, MAX, DCOL = F, F + 1, F + 2
    with ExitStack() as ctx:
        def sb(name, shape, dt):
            return ctx.enter_context(nc.sbuf_tensor(name, shape, dt))

        def ps(name, shape):
            return ctx.enter_context(nc.psum_tensor(name, shape, F32))

        def sem(name):
            return ctx.enter_context(nc.semaphore(name))

        first = sb("first", [WN, 10, ST], F32)
        later = sb("later", [CH, CH], F32)
        ones = sb("g_ones", [CH, CH], F32)
        si = sb("si", [CH, 1], I32)
        di = sb("di", [CH, 1], I32)
        ef = sb("g_ef", [CH, FE], F32)
        efj = sb("g_efj", [CH, FE], F32)
        hg = sb("hg", [CH, ROW], F32)
        sg = sb("sg", [CH, ST], F32)
        sn = sb("sn", [CH, ST], F32)
        col = sb("col", [CH, 8], F32)
        arg = sb("arg", [CH, 2], F32)
        ex = sb("g_ex", [CH, 2], F32)
        rep = sb("rep", [CH, 2, CH], F32)
        row = sb("row", [CH, 2, CH], F32)
        eq = sb("eq", [CH, CH], F32)
        m1 = sb("m1", [CH, CH], F32)
        m2 = sb("m2", [CH, CH], F32)
        wt = sb("g_wt", [CH, CH], F32)
        dup = sb("dup", [CH, CH], F32)
        so = sb("so", [CH, 1], I32)
        row_ps = ps("row_ps", [CH, 2, CH])
        sum_ps = ps("sum_ps", [CH, F + 1])
        st = sb("st", [WN, ST], F32)
        rden = sb("g_rden", [WN, 2], F32)
        agg = sb("g_agg", [WN, F], F32)
        aggT = sb("g_aggT", [128, KF, WN], F32)
        ob = sb("g_ob", [WN, F], F32)
        aggT_ps = ps("g_aggT_ps", [128, KF, WN])
        z_ps = ps("g_z_ps", [WN, F])

        made = sem("g_made")
        first_out = sem("g_first_out")
        loaded = sem("g_loaded")
        gathered = sem("g_gathered")
        rows_turned = sem("g_rows_turned")
        rep_made = sem("g_rep_made")
        first_ready = sem("g_first_ready")
        arg_made = sem("g_arg_made")
        ex_made = sem("g_ex_made")
        wt_made = sem("g_wt_made")
        summed = sem("g_summed")
        v = sem("g_v")
        new_state = sem("g_new_state")
        scattered = sem("g_scattered")
        state_in = sem("g_state_in")
        agg_made = sem("g_agg_made")
        agg_turned = sem("g_agg_turned")
        aggT_kept = sem("g_aggT_kept")
        z_made = sem("g_z_made")
        den_made = sem("g_den_made")
        ob_made = sem("g_ob_made")
        pool_at = sem("g_pool_at")
        stored = sem("g_stored")

        chunk_ops = 14
        def if_unsorted(engine, body):
            bad = engine.value_load(flag[0:1, 0:1], min_val=0, max_val=1)
            with engine.If(bad == 1):
                body()
            with engine.Else():
                engine.nop()

        with nc.Block() as block:
            @block.sync
            def _(sp):
                def body():
                    with sp.Fori(0, 5) as b:
                        sp.wait_ge(first_ready, b + 1)
                        sp.dma_start(state.rearrange("(t p) f -> p t f", p=WN)[:, bass.ds(10 * b, 10), :],
                                     first[:]).then_inc(first_out, 16)
                    sp.wait_ge(first_out, 16 * 5)
                    with sp.Fori(0, NC) as c:
                        sp.wait_ge(scattered, 16 * c)
                        sp.dma_start(si[:], src[bass.ds(CH * c, CH)].rearrange("(p a) -> p a", a=1)).then_inc(loaded, 16)
                        sp.dma_start(di[:], dst[bass.ds(CH * c, CH)].rearrange("(p a) -> p a", a=1)).then_inc(loaded, 16)
                        sp.dma_start(ef[:], edge_attr[bass.ds(CH * c, CH), :]).then_inc(loaded, 16)
                    sp.wait_ge(scattered, 16 * NC)
                    with sp.Fori(0, NW) as w:
                        sp.wait_ge(ob_made, w)
                        sp.dma_start(st[:], state[bass.ds(WN * w, WN), :]).then_inc(state_in, 16)
                        sp.wait_ge(ob_made, w + 1)
                        sp.dma_start(out[bass.ds(WN * w, WN), :], ob[:]).then_inc(stored, 16)
                    sp.wait_ge(stored, 16 * NW)

                if_unsorted(sp, body)

            @block.gpsimd
            def _(pool):
                def body():
                    nc.gpsimd.memset(later[:], 1.0).then_inc(made, 1)
                    pool.wait_ge(made, 1)
                    nc.gpsimd.affine_select(out=later[:], in_=later[:], compare_op=ALU.is_gt, fill=0.0, base=0,
                                            pattern=[[1, CH]], channel_multiplier=-1).then_inc(made, 1)
                    pool.wait_ge(first_out, 16 * 5)
                    with pool.Fori(0, NC) as c:
                        pool.wait_ge(loaded, 48 * c + 48)
                        pool.sem_inc(pool_at, 1)
                        pool.indirect_dma_start(out=hg[:], **on_row(table, si[:])).then_inc(gathered, 16)
                        pool.indirect_dma_start(out=sg[:], **on_row(state, di[:])).then_inc(gathered, 16)
                        pool.wait_ge(new_state, 4 * c + 4)
                        pool.sem_inc(pool_at, 1)
                        pool.indirect_dma_start(out=state, out_offset=bass.IndirectOffsetOnAxis(ap=so[:], axis=0),
                                                in_=sn[:], in_offset=None, bounds_check=N - 1,
                                                oob_is_err=False).then_inc(scattered, 16)

                if_unsorted(pool, body)

            @block.tensor
            def _(pe):
                def body():
                    with pe.Fori(0, NC) as c:
                        pe.wait_ge(rep_made, 2 * c + 2)
                        for s in range(2):
                            mm = nc.tensor.transpose(row_ps[:, s, :], rep[:, s, :], ident[0:CH, 0:CH])
                        mm.then_inc(rows_turned, 1)
                        pe.wait_ge(wt_made, c + 1)
                        nc.tensor.matmul(sum_ps[:], wt[:], hg[:, 0:F + 1], start=True, stop=True).then_inc(summed, 1)
                    with pe.Fori(0, NW) as w:
                        pe.wait_ge(agg_made, w + 1)
                        for k in range(KF):
                            mm = nc.tensor.transpose(aggT_ps[:, k, :], agg[:, 128 * k:128 * k + 128], ident[0:WN, 0:WN])
                        mm.then_inc(agg_turned, 1)
                        pe.wait_ge(aggT_kept, w + 1)
                        for k in range(KF):
                            mm = nc.tensor.matmul(z_ps[:], aggT[:, k, :], WT[:, k, :], start=(k == 0), stop=(k == KF - 1))
                        mm.then_inc(z_made, 1)

                if_unsorted(pe, body)

            @block.scalar
            def _(act):
                def body():
                    with act.Fori(0, NC) as c:
                        act.wait_ge(arg_made, 2 * c + 2)
                        nc.scalar.activation(ex[:], arg[:], ACT.Exp).then_inc(ex_made, 1)
                    with act.Fori(0, NW) as w:
                        act.wait_ge(agg_turned, w + 1)
                        nc.scalar.copy(aggT[:].rearrange("p k n -> p (k n)"),
                                       aggT_ps[:].rearrange("p k n -> p (k n)")).then_inc(aggT_kept, 1)

                if_unsorted(act, body)

            @block.vector
            def _(dve):
                def body():
                    nc.vector.memset(ones[:], 1.0).then_inc(v, 1)
                    nc.vector.memset(first[:], 0.0).then_inc(v, 1)
                    dve.wait_ge(v, 2)
                    nc.vector.memset(first[:, :, MAX], -BIG).then_inc(v, 1)
                    dve.wait_ge(v, 3)
                    dve.wait_ge(made, 2)
                    with dve.Fori(0, 5) as b:
                        dve.wait_ge(first_out, 16 * b)
                        nc.vector.tensor_copy(first[:, :, DCOL], d_all[:, bass.ds(10 * b, 10)]).then_inc(first_ready, 1)
                    with dve.Fori(0, NC) as c:
                        n = [3]

                        def then(ins):
                            n[0] += 1
                            ins.then_inc(v, 1)
                            dve.wait_ge(v, chunk_ops * c + n[0])

                        dstf, ee, r, lg, l, mx, m_new, twice = (col[:, i:i + 1] for i in range(8))
                        dve.wait_ge(loaded, 48 * c + 48)
                        dve.wait_ge(gathered, 32 * c + 32)
                        then(nc.vector.tensor_copy(dstf, di[:]))
                        then(nc.vector.tensor_tensor_reduce(efj[:], ef[:], ae_bc[:], 1.0, 0.0, ALU.mult, ALU.add, ee))
                        then(nc.vector.tensor_tensor(r, ee, hg[:, S:S + 1], ALU.add))
                        then(nc.vector.tensor_tensor(lg, r, sg[:, DCOL:DCOL + 1], ALU.add))
                        then(nc.vector.scalar_tensor_tensor(out=l, in0=lg, scalar=SLOPE, in1=lg, op0=ALU.mult,
                                                            op1=ALU.max))
                        nc.vector.tensor_scalar(rep[:, 0, :], ones[:], dstf, None, ALU.mult).then_inc(rep_made, 1)
                        nc.vector.tensor_scalar(rep[:, 1, :], ones[:], l, None, ALU.mult).then_inc(rep_made, 1)
                        dve.wait_ge(rows_turned, c + 1)
                        then(nc.vector.tensor_copy(row[:], row_ps[:]))
                        then(nc.vector.tensor_scalar(eq[:], row[:, 0, :], dstf, None, ALU.is_equal))
                        then(nc.vector.tensor_scalar(m1[:], eq[:], -1.0, BIG, ALU.add, ALU.mult))
                        then(nc.vector.tensor_tensor(m2[:], m1[:], row[:, 1, :], ALU.add))
                        then(nc.vector.tensor_reduce(mx, m2[:], AX.X, ALU.max))
                        then(nc.vector.tensor_tensor(m_new, mx, sg[:, MAX:MAX + 1], ALU.max))
                        nc.vector.tensor_tensor(arg[:, 0:1], l, m_new, ALU.subtract).then_inc(arg_made, 1)
                        nc.vector.tensor_tensor(arg[:, 1:2], sg[:, MAX:MAX + 1], m_new, ALU.subtract).then_inc(arg_made, 1)
                        then(nc.vector.tensor_tensor(dup[:], eq[:], later[:], ALU.mult))
                        then(nc.vector.tensor_reduce(twice, dup[:], AX.X, ALU.max))
                        nc.vector.scalar_tensor_tensor(out=so[:], in0=twice, scalar=float(2 * N), in1=dstf,
                                                       op0=ALU.mult, op1=ALU.add).then_inc(new_state, 1)
                        nc.vector.tensor_copy(sn[:, MAX:MAX + 1], m_new).then_inc(new_state, 1)
                        nc.vector.tensor_copy(sn[:, DCOL:DCOL + 1], sg[:, DCOL:DCOL + 1]).then_inc(new_state, 1)
                        dve.wait_ge(ex_made, c + 1)
                        nc.vector.tensor_scalar(wt[:], eq[:], ex[:, 0:1], None, ALU.mult).then_inc(wt_made, 1)
                        dve.wait_ge(summed, c + 1)
                        then(nc.vector.scalar_tensor_tensor(out=sn[:, 0:F + 1], in0=sg[:, 0:F + 1], scalar=ex[:, 1:2],
                                                            in1=sum_ps[:], op0=ALU.mult, op1=ALU.add))
                        nc.vector.sem_inc(new_state, 1)
                        assert n[0] == chunk_ops + 3
                    with dve.Fori(0, NW) as w:
                        dve.wait_ge(state_in, 16 * w + 16)
                        nc.vector.tensor_scalar(rden[:, 0:1], st[:, DEN:DEN + 1], TINY, None,
                                                ALU.max).then_inc(den_made, 1)
                        dve.wait_ge(den_made, 2 * w + 1)
                        nc.vector.reciprocal(rden[:, 1:2], rden[:, 0:1]).then_inc(den_made, 1)
                        dve.wait_ge(den_made, 2 * w + 2)
                        nc.vector.tensor_scalar(agg[:], st[:, 0:F], rden[:, 1:2], None, ALU.mult).then_inc(agg_made, 1)
                        dve.wait_ge(z_made, w + 1)
                        dve.wait_ge(stored, 16 * w)
                        nc.vector.tensor_tensor(ob[:], z_ps[:], x_all[:, bass.ds(w, 1), :].rearrange("p a f -> p (a f)"),
                                                ALU.add).then_inc(ob_made, 1)

                if_unsorted(dve, body)


def kernel(x, src, dst, edge_attr_64, L0_gnn_W, L0_gnn_A):
    import numpy as np
    import concourse.bacc as bacc
    from concourse.bass_utils import run_bass_kernel_spmd

    nc = bacc.Bacc("TRN2", target_bir_lowering=False, num_devices=1)
    given = {"x": x, "src": src, "dst": dst, "edge_attr": edge_attr_64, "W": L0_gnn_W, "A": L0_gnn_A}
    arrays, aps = {}, {}
    for name, a in given.items():
        a = np.ascontiguousarray(a)
        arrays[f"in_{name}"] = a
        aps[name] = nc.dram_tensor(f"in_{name}", a.shape, mybir.dt.from_np(a.dtype), kind="ExternalInput").ap()
    aps["out"] = nc.dram_tensor("out", tuple(x.shape), F32, kind="ExternalOutput").ap()
    gnn_kernel(nc, **aps)
    return run_bass_kernel_spmd(nc, [arrays], core_ids=[0]).results[0]["out"]
```

```python
from contextlib import ExitStack

import concourse.bass as bass
from concourse import mybir
from concourse.alu_op_type import AluOpType as ALU

ACT = mybir.ActivationFunctionType
F32 = mybir.dt.float32
BF16 = mybir.dt.bfloat16
I32 = mybir.dt.int32
I16 = mybir.dt.int16
AX = mybir.AxisListType

SLOPE = 0.2
EPS = 1e-5
BIG = 2.0 ** 100
TINY = 1e-30
UNROLL = 4
HALO = 64
SHARED = 6
PAD_NODE = 10 ** 6


def on_row(table, index_column):
    return dict(in_=table, in_offset=bass.IndirectOffsetOnAxis(ap=index_column, axis=0), out_offset=None)


class Step:

    def __init__(self, c, i=None):
        self.c, self.i = c, i

    def times(self, m, add=0):
        rest = m * self.c + add
        if self.i is None:
            return rest
        assert rest >= 0, "a wait's value stays above zero"
        return UNROLL * m * self.i + rest

    def turns(self, n, d=0):
        rest = (self.c + d) // n
        return rest if self.i is None else UNROLL // n * self.i + rest

    def plus(self, d):
        return Step(self.c + d, self.i)


def wait(engine, semaphore, value):
    if not isinstance(value, int) or value > 0:
        engine.wait_ge(semaphore, value)


def gnn_kernel(nc, x, src, dst, edge_attr, W, A, out):
    N, F = x.shape
    E, FE = edge_attr.shape
    WN = CH = 125
    NW, NC = N // WN, E // CH
    assert N == NW * WN and E == NC * CH and F == 256
    KF = F // 128
    ONE, S, ROW = F, F + 1, F + 2
    NT, GRP = 10, 5
    NS = NW // NT
    NP, ON_PE = 3, 6
    ON_DVE = NT - ON_PE
    NH = 3
    FRONT_P = 112
    assert ON_PE == 2 * NP
    ST = F + 3

    G = NC // NW
    NB = NW + 1
    FRONT = 192
    PADDED = FRONT + CH * (NB * G - 2) + CH + HALO
    BACK = PADDED - FRONT - E
    BACK_ROWS = next(r for r in (16, 15, 14, 13, 12, 11, 10, 9, 8) if BACK % r == 0 and BACK // r + FRONT // 16 <= 256)
    EP = E // CH
    assert FRONT >= CH + HALO
    src_rows = src.rearrange("(b c p) -> c b p", b=10, p=CH)
    dst_rows = dst.rearrange("(b c p) -> c b p", b=10, p=CH)
    RB = NC // 10
    RB_P = RB // 16 * 16

    dst_pad = nc.dram_tensor("dst_pad", (PADDED,), I32).ap()
    dst16_pad = nc.dram_tensor("dst16_pad", (NB * G * CH,), I16).ap()
    r_pad = nc.dram_tensor("r_pad", (PADDED,), F32).ap()
    table = nc.dram_tensor("node_table", (N, ROW), F32).ap()
    state = nc.dram_tensor("node_state", (N, ST), F32).ap()

    with ExitStack() as top:
        def sb(name, shape, dt, where=top):
            return where.enter_context(nc.sbuf_tensor(name, shape, dt))

        def ps(name, shape, where=top):
            return where.enter_context(nc.psum_tensor(name, shape, F32))

        def sem(name, where=top):
            return where.enter_context(nc.semaphore(name))

        x_all = sb("x_all", [WN, NW, F], F32)
        d_all = sb("d_all", [WN, NW], F32)
        d3 = sb("d3", [WN, NW + 3, 3], BF16)
        node_id = sb("node_id", [WN, NW + 3], F32)
        iota = sb("iota", [CH, 3 * WN], F32)
        src_all = sb("src_all", [CH, NC], I32)
        rel_all = sb("rel_all", [CH, NB * G], F32)
        flag = sb("flag", [1, 1], I32)
        ae_bc = sb("ae_bc", [WN, FE], F32)
        WT = sb("WT", [128, KF, F], F32)
        ident = sb("ident", [128, 128], F32)

        with ExitStack() as ctx:
            hs = sb("hs", [WN, NH, NT, ROW], F32, ctx)
            hT = sb("hT", [128, NP, 2, KF, WN], F32, ctx)
            w_sb = sb("w_sb", [128, KF, F], F32, ctx)
            a_col = sb("a_col", [128, 2 * KF], F32, ctx)
            a_rep = sb("a_rep", [128, 2 * KF, WN], F32, ctx)
            ones = sb("ones", [128, WN], F32, ctx)
            uv_col = sb("uv_col", [128, KF, 2], F32, ctx)
            uv_bc = sb("uv_bc", [WN, 2, F], F32, ctx)
            dots = sb("dots", [WN, ON_DVE], F32, ctx)
            junk = sb("junk", [WN, 2, F], F32, ctx)
            stats = sb("stats", [WN, NT, 6], F32, ctx)
            nt = {k: sb(f"nt_{k}", [WN, NT], F32, ctx) for k in (
                "sum", "gap", "sq", "gap2", "sq_all", "var", "std", "inv", "ratio", "step")}
            rstd = sb("rstd", [WN, 2, NT], F32, ctx)
            shift = sb("shift", [WN, 2, NT], F32, ctx)
            rest = sb("rest", [WN, 2, NW], F32, ctx)
            rows = sb("rows", [RB, 2, 10, CH], I32, ctx)
            rows_f = sb("rows_f", [RB, 2, 10, CH], F32, ctx)
            first_node = sb("first_node", [CH, NB, G], I32, ctx)
            node_i = sb("node_i", [WN, NW + 3], I32, ctx)
            iota_i = sb("iota_i", [CH, 3 * WN], I32, ctx)
            pad_i = sb("pad_i", [16, 256], I32, ctx)
            pad_f = sb("pad_f", [16, 256], F32, ctx)
            pad_16 = sb("pad_16", [G, CH], I16, ctx)
            line = sb("line", [CH, EP + HALO], I32, ctx)
            line_f = sb("line_f", [CH, EP + HALO], F32, ctx)
            line16 = sb("line16", [CH, EP], I16, ctx)
            rise = sb("rise", [CH, 2, EP], F32, ctx)
            low = sb("low", [CH, 6], F32, ctx)
            bad = sb("bad", [CH, 8], F32, ctx)
            bad_row = sb("bad_row", [1, 2], F32, ctx)
            turn_ps = ps("turn_ps", [128, NP + 1, 512], ctx)
            dots_ps = ps("dots_ps", [WN, ON_PE, 2], ctx)
            wt_ps = ps("wt_ps", [128, KF * F], ctx)
            uv_bc_ps = ps("uv_bc_ps", [WN, 2, F], ctx)
            small_ps = ps("small_ps", [128, 512], ctx)
            uv_ps = small_ps[:, 0:2 * KF]
            bad_ps = small_ps[0:1, 128:128 + CH]
            turned_rows = [turn_ps[:, NP, :], uv_bc_ps[:].rearrange("p s f -> p (s f)"), wt_ps[:], small_ps[:]]

            weights_in = sem("weights_in", ctx)
            x_in = [[sem(f"x_in{h}{j}", ctx) for j in range(2)] for h in range(2)]
            hs_set = sem("hs_set", ctx)
            ident_made = sem("ident_made", ctx)
            uv_summed = sem("uv_summed", ctx)
            uv_kept = sem("uv_kept", ctx)
            wt_turned = sem("wt_turned", ctx)
            wt_kept = sem("wt_kept", ctx)
            src_kept = sem("src_kept", ctx)
            chain = sem("chain", ctx)
            stat_done = sem("stat_done", ctx)
            var_made = sem("var_made", ctx)
            std_made = sem("std_made", ctx)
            shift_made = sem("shift_made", ctx)
            h_made = sem("h_made", ctx)
            h_turned = sem("h_turned", ctx)
            hT_kept = sem("hT_kept", ctx)
            ones_made = sem("ones_made", ctx)
            a_rep_made = sem("a_rep_made", ctx)
            uv_bc_summed = sem("uv_bc_summed", ctx)
            uv_bc_kept = sem("uv_bc_kept", ctx)
            dots_done = sem("dots_done", ctx)
            dots_made = sem("dots_made", ctx)
            s_kept = sem("s_kept", ctx)
            dots_moved = sem("dots_moved", ctx)
            dots_free = sem("dots_free", ctx)
            table_out = [[sem(f"table_out{h}{j}", ctx) for j in range(2)] for h in range(NH)]
            last_out = sem("last_out", ctx)

            rows_in = [sem(f"rows_in{s}", ctx) for s in range(2)]
            rows_cast = [sem(f"rows_cast{s}", ctx) for s in range(2)]
            rows_turned = sem("rows_turned", ctx)
            rows_kept = sem("rows_kept", ctx)
            iotas = sem("iotas", ctx)
            pads_made = sem("pads_made", ctx)
            pads_out = sem("pads_out", ctx)
            line_set = sem("line_set", ctx)
            line_in = sem("line_in", ctx)
            line16_made = sem("line16_made", ctx)
            line16_out = sem("line16_out", ctx)
            rises = sem("rises", ctx)
            lows = sem("lows", ctx)
            bads = sem("bads", ctx)
            bad_turned = sem("bad_turned", ctx)
            split = sem("split", ctx)

            x_tiles = x.rearrange("(t p) f -> p t f", p=WN)
            table_tiles = table.rearrange("(t p) f -> p t f", p=WN)

            def steps(engine, one):
                for k in range(NS):
                    one(Step(k))

            with nc.Block() as block:
                @block.sync
                def _(sp):
                    def load(k):
                        for j in range(2):
                            t = NT * k + GRP * j
                            done = x_in[k % 2][j]
                            wait(sp, done, 32 * (k // 2))
                            for p, n in ((0, FRONT_P), (FRONT_P, WN - FRONT_P)):
                                sp.dma_start(x_all[p:p + n, t:t + GRP, :], x_tiles[p:p + n, t:t + GRP, :]).then_inc(done, 16)

                    load(0)
                    load(1)
                    sp.wait_ge(line_set, 1)
                    for p, n in ((0, FRONT_P), (FRONT_P, CH - 1 - FRONT_P)):
                        sp.dma_start(line[p:p + n, :], bass.AP(tensor=dst.tensor, offset=dst.offset + EP * p,
                                                               ap=[[EP, n], [1, EP + HALO]])).then_inc(line_in, 16)
                    sp.dma_start(line[CH - 1:CH, 0:EP], dst[E - EP:E].rearrange("(p k) -> p k", p=1)).then_inc(line_in, 16)
                    line_of = lambda a: a.rearrange("(p k) -> p k", p=CH)
                    back = lambda a: a[FRONT + E:PADDED].rearrange("(p k) -> p k", p=BACK_ROWS)
                    front = lambda a: a[0:FRONT].rearrange("(p k) -> p k", p=16)
                    sp.dma_start(line_of(dst_pad[FRONT:FRONT + E]), line_of(dst)).then_inc(pads_out, 16)
                    sp.wait_ge(pads_made, 4)
                    fc, bc = FRONT // 16, BACK // BACK_ROWS
                    sp.dma_start(front(dst_pad), pad_i[:, 0:fc]).then_inc(pads_out, 16)
                    sp.dma_start(back(dst_pad), pad_i[0:BACK_ROWS, fc:fc + bc]).then_inc(pads_out, 16)
                    sp.dma_start(front(r_pad), pad_f[:, 0:fc]).then_inc(pads_out, 16)
                    sp.dma_start(back(r_pad), pad_f[0:BACK_ROWS, 0:bc]).then_inc(pads_out, 16)
                    sp.dma_start(dst16_pad[0:CH].rearrange("(p k) -> p k", p=1), pad_16[0:1, :]).then_inc(pads_out, 16)
                    sp.dma_start(dst16_pad[CH + E:].rearrange("(p k) -> p k", k=CH), pad_16[1:G, :]).then_inc(pads_out, 16)
                    load(2)
                    for k in range(3, NS):
                        load(k)
                    sp.wait_ge(pads_out, 16 * 7)
                    sp.wait_ge(line16_made, 1)
                    sp.dma_start(line_of(dst16_pad[CH:CH + E]), line16[:]).then_inc(line16_out, 16)
                    sp.wait_ge(s_kept, NS)
                    for p, n in ((0, FRONT_P), (FRONT_P, WN - FRONT_P)):
                        sp.dma_start(table_tiles[p:p + n, NW - NT:NW - NT + ON_PE, :],
                                     hs[p:p + n, (NS - 1) % NH, 0:ON_PE, :]).then_inc(last_out, 16)
                    sp.wait_ge(line16_out, 16)
                    sp.wait_ge(last_out, 32)

                @block.gpsimd
                def _(pool):
                    nc.gpsimd.memset(ident[:], 0.0).then_inc(ident_made, 1)
                    pool.wait_ge(ident_made, 1)
                    nc.gpsimd.affine_select(out=ident[:], in_=ident[:], compare_op=ALU.not_equal, fill=1.0, base=0,
                                            pattern=[[-1, 128]], channel_multiplier=1).then_inc(ident_made, 1)
                    nc.gpsimd.memset(pad_i[:], PAD_NODE).then_inc(iotas, 1)
                    nc.gpsimd.memset(pad_f[:], 0.0).then_inc(pads_made, 1)
                    nc.gpsimd.memset(pad_16[:], -1).then_inc(pads_made, 1)
                    pool.wait_ge(iotas, 1)
                    nc.gpsimd.memset(pad_i[:, 0:FRONT // 16], -PAD_NODE).then_inc(pads_made, 2)
                    nc.gpsimd.iota(first_node[:], pattern=[[WN, NB], [0, G]], base=0,
                                   channel_multiplier=0).then_inc(iotas, 1)
                    nc.gpsimd.iota(node_i[:], pattern=[[WN, NW + 3]], base=-WN, channel_multiplier=1).then_inc(iotas, 1)
                    nc.gpsimd.iota(iota_i[:], pattern=[[1, 3 * WN]], base=-WN, channel_multiplier=0).then_inc(iotas, 1)
                    pool.wait_ge(iotas, 4)
                    nc.gpsimd.tensor_copy(node_id[:], node_i[:]).then_inc(iotas, 1)
                    nc.gpsimd.tensor_copy(iota[:], iota_i[:]).then_inc(iotas, 1)
                    for s in range(2):
                        pool.wait_ge(rows_in[s], 32)
                        nc.gpsimd.tensor_copy(rows_f[:, s], rows[:, s]).then_inc(rows_cast[s], 1)

                    def one(k):
                        h = k.c % NH
                        for j, (t0, t1, ready, value) in enumerate((
                                (0, ON_PE, s_kept, k.times(1, 1)),
                                (ON_PE, NT, dots_made, k.times(2 * ON_DVE, 2 * ON_DVE)))):
                            if k.c == NS - 1 and ready is s_kept:
                                continue
                            wait(pool, ready, value)
                            pool.dma_start(table_tiles[:, bass.ds(k.times(NT, t0), t1 - t0), :],
                                           hs[:, h, t0:t1, :]).then_inc(table_out[h][j], 16)

                    one(Step(0))
                    pool.wait_ge(line_in, 48)
                    nc.gpsimd.tensor_copy(line16[:], line[:, 0:EP]).then_inc(line16_made, 1)
                    nc.gpsimd.tensor_copy(line_f[:], line[:]).then_inc(line16_made, 1)
                    pool.wait_ge(line16_made, 2)
                    nc.gpsimd.tensor_tensor(rise[:, 0], line_f[:, 1:EP + 1], line_f[:, 0:EP], ALU.subtract).then_inc(rises, 1)
                    nc.gpsimd.tensor_tensor(rise[:, 1], line_f[:, HALO:EP + HALO], line_f[:, 0:EP],
                                            ALU.subtract).then_inc(rises, 1)
                    for k in range(1, NS):
                        one(Step(k))
                    for k in range(NS - NH, NS):
                        for j in range(2):
                            if (k, j) != (NS - 1, 0):
                                pool.wait_ge(table_out[k % NH][j], 16 * (k // NH + 1))

                @block.tensor
                def _(pe):
                    pe.wait_ge(ident_made, 2)
                    pe.wait_ge(weights_in, 48)
                    for f in range(KF):
                        for c in range(KF):
                            mm = nc.tensor.matmul(uv_ps[:, 2 * f:2 * f + 2], w_sb[:, c, 128 * f:128 * f + 128],
                                                  a_col[:, c::KF], start=(c == 0), stop=(c == KF - 1))
                    mm.then_inc(uv_summed, 1)
                    for s in range(2):
                        pe.wait_ge(a_rep_made, KF * (s + 1))
                        for c in range(KF):
                            mm = nc.tensor.matmul(uv_bc_ps[:, s, :], a_rep[:, KF * s + c, :], w_sb[:, c, :],
                                                  start=(c == 0), stop=(c == KF - 1))
                    mm.then_inc(uv_bc_summed, 1)
                    for a in range(KF):
                        for b in range(KF):
                            at = 128 * (KF * a + b)
                            mm = nc.tensor.transpose(wt_ps[:, at:at + 128], w_sb[:, b, 128 * a:128 * a + 128], ident[:])
                    mm.then_inc(wt_turned, 1)

                    def turn(k, q):
                        wait(pe, h_made, k.times(NT, 2 * q + 2))
                        for t in range(2):
                            for f in range(KF):
                                at = WN * (KF * t + f)
                                mm = nc.tensor.transpose(turn_ps[:, q, at:at + WN],
                                                         hs[:, k.c % NH, 2 * q + t, 128 * f:128 * f + 128],
                                                         ident[0:WN, 0:WN])
                        mm.then_inc(h_turned, 1)

                    def dots(k, q):
                        wait(pe, hT_kept, k.times(NP, q + 1))
                        if q == 0:
                            wait(pe, dots_free, k.times(1, 1))
                        for t in range(2):
                            for f in range(KF):
                                mm = nc.tensor.matmul(dots_ps[:, 2 * q + t, :], hT[:, q, t, f, :], uv_col[:, f, :],
                                                      start=(f == 0), stop=(f == KF - 1))
                        if q == NP - 1:
                            mm.then_inc(dots_done, 1)

                    pe.wait_ge(uv_kept, 1)

                    def turn_rows():
                        pe.wait_ge(wt_kept, 1)
                        pe.wait_ge(uv_bc_kept, 1)
                        for q in range(4):
                            pe.wait_ge(rows_cast[q // 2], 1)
                            for b in range(5):
                                mm = nc.tensor.transpose(turned_rows[q][0:CH, RB * b:RB * b + RB],
                                                         rows_f[:, q // 2, 5 * (q % 2) + b, :], ident[0:RB, 0:RB])
                            mm.then_inc(rows_turned, 1)

                    def one(k):
                        turn(k, 0)
                        turn(k, 1)
                        dots(k, 0)
                        turn(k, 2)
                        dots(k, 1)
                        dots(k, 2)

                    for k in range(NS):
                        if k == 2:
                            turn_rows()
                        one(Step(k))
                    pe.wait_ge(bads, 3)
                    nc.tensor.transpose(bad_ps, bad[:, 6:7], ident[0:CH, 0:CH]).then_inc(bad_turned, 1)

                @block.scalar
                def _(act):
                    act.dma_start(w_sb[:], W.rearrange("(c p) i -> p c i", p=128)).then_inc(weights_in, 16)
                    act.dma_start(a_col[:], A[0, 0:2 * F].rearrange("(c p) -> p c", p=128), allow_slow_non_contiguous=True).then_inc(weights_in, 16)
                    act.dma_start(ae_bc[:], A[0, 2 * F:2 * F + FE].partition_broadcast(WN)).then_inc(weights_in, 16)
                    for s, listed in ((0, src_rows), (1, dst_rows)):
                        for p, n in ((0, RB_P), (RB_P, RB - RB_P)):
                            act.dma_start(rows[p:p + n, s], listed[p:p + n]).then_inc(rows_in[s], 16)
                    def root(k):
                        wait(act, var_made, k.times(1, 1))
                        nc.scalar.activation(nt["std"][:], nt["var"][:], ACT.Sqrt).then_inc(std_made, 1)

                    def relu(k, j):
                        h = k.c % 2
                        if j == 0:
                            wait(act, shift_made, k.times(1, 1))
                            for part in range(2):
                                wait(act, table_out[k.c % NH][part], 16 * (k.c // NH))
                        nc.scalar.activation(hs[:, k.c % NH, j, 0:F], x_all[:, bass.ds(k.times(NT, j), 1), :]
                                             .rearrange("p a f -> p (a f)"), ACT.Relu,
                                             bias=shift[:, h, j:j + 1], scale=rstd[:, h, j:j + 1]).then_inc(h_made, 1)

                    def move(k, q):
                        wait(act, h_turned, k.times(NP, q + 1))
                        nc.scalar.copy(hT[:, q].rearrange("p t f n -> p (t f n)"),
                                       turn_ps[:, q, 0:2 * KF * WN]).then_inc(hT_kept, 1)

                    def one(k):
                        for j in range(2, 8):
                            relu(k, j)
                            if j in (3, 5):
                                move(k, (j - 3) // 2)
                            if j == 7 and k.c + 1 < NS:
                                root(k.plus(1))
                        move(k, 2)
                        relu(k, 8)
                        relu(k, 9)
                        if k.c + 1 < NS:
                            relu(k.plus(1), 0)
                            relu(k.plus(1), 1)
                        wait(act, dots_done, k.times(1, 1))
                        nc.scalar.copy(hs[:, k.c % NH, 0:ON_PE, S], dots_ps[:, :, 0]).then_inc(s_kept, 1)
                        nc.scalar.copy(d_all[:, bass.ds(k.times(NT), ON_PE)], dots_ps[:, :, 1]).then_inc(dots_free, 1)

                    act.wait_ge(ones_made, 1)
                    act.wait_ge(weights_in, 48)
                    for c in range(2 * KF):
                        nc.scalar.mul(a_rep[:, c, :], ones[:], a_col[:, c:c + 1]).then_inc(a_rep_made, 1)
                    root(Step(0))
                    act.wait_ge(hs_set, 1)
                    relu(Step(0), 0)
                    relu(Step(0), 1)
                    act.wait_ge(wt_turned, 1)
                    nc.scalar.copy(WT[:].rearrange("p a f -> p (a f)"), wt_ps[:]).then_inc(wt_kept, 1)
                    act.sem_inc(dots_free, 1)
                    steps(act, one)
                    for q in range(2):
                        act.wait_ge(rows_turned, q + 1)
                        nc.scalar.copy(src_all[:, 5 * RB * q:5 * RB * (q + 1)],
                                       turned_rows[q][0:CH, 0:5 * RB]).then_inc(src_kept, 1)

                @block.vector
                def _(dve):
                    links = 9

                    def dot(k, j, s):
                        if s == 0:
                            wait(dve, h_made, k.times(NT, ON_PE + j + 1))
                        if 2 * j + s >= 2:
                            wait(dve, dots_made, k.times(2 * ON_DVE, 2 * j + s - 1))
                        kept = dots[:, j:j + 1] if s else hs[:, k.c % NH, ON_PE + j, S:S + 1]
                        nc.vector.tensor_tensor_reduce(junk[:, s, :], hs[:, k.c % NH, ON_PE + j, 0:F], uv_bc[:, s, :],
                                                       1.0, 0.0, ALU.mult, ALU.add, kept).then_inc(dots_made, 1)

                    def edges():
                        dve.wait_ge(rows_kept, 1)
                        dve.wait_ge(iotas, 2)
                        base = first_node[:].rearrange("p k g -> p (k g)")
                        for q in range(2):
                            dve.wait_ge(rows_turned, 3 + q)
                            cols = slice(1 + 5 * RB * q, 1 + 5 * RB * (q + 1))
                            nc.vector.tensor_tensor(rel_all[:, cols], turned_rows[2 + q][0:CH, 0:5 * RB], base[:, cols],
                                                    ALU.subtract).then_inc(rows_kept, 1)
                        dve.wait_ge(rows_kept, 3)
                        dve.wait_ge(rises, 2)
                        rel = rel_all[:].rearrange("p (k g) -> p k g", g=G)
                        for n, (what, op) in enumerate((
                                (rel[:, 1:NB, 0], ALU.min), (rel[:, 0:NW, SHARED + 1], ALU.min),
                                (rel[:, 0:NW, G - SHARED], ALU.max), (rel[:, 0:NW, G - 1], ALU.max),
                                (rise[:, 0], ALU.min), (rise[:, 1], ALU.min))):
                            nc.vector.tensor_reduce(low[:, n:n + 1], what, AX.X, op).then_inc(lows, 1)
                        dve.wait_ge(lows, 6)
                        for n, (m, a) in enumerate(((-1, -WN), (-1, 0), (1, 1 - WN), (1, 1 - 2 * WN), (-1, 0), (-1, 1))):
                            nc.vector.tensor_scalar(bad[:, n:n + 1], low[:, n:n + 1], float(m), float(a), ALU.mult,
                                                    ALU.add).then_inc(lows, 1)
                        dve.wait_ge(lows, 12)
                        nc.vector.tensor_reduce(bad[:, 6:7], bad[:, 0:6], AX.X, ALU.max).then_inc(bads, 3)

                    def normal(k, dots_of=None):
                        def between(n):
                            if dots_of is not None:
                                dot(dots_of, n // 2, n % 2)

                        h = k.c % 2
                        for j in range(NT):
                            if j % GRP == 0:
                                wait(dve, x_in[h][j // GRP], 32 * k.turns(2, 2))
                            nc.vector.bn_stats(stats[:, j, :], x_all[:, bass.ds(k.times(NT, j), 1), :]
                                               .rearrange("p a f -> p (a f)")).then_inc(stat_done, 1)
                        wait(dve, stat_done, k.times(NT, NT))
                        n = [0]

                        def link(ins):
                            ins().then_inc(chain, 1)
                            n[0] += 1
                            return n[0]

                        def reads(link_number):
                            wait(dve, chain, k.times(links, link_number))

                        mean_e, sq_e, mean_o, sq_o = (stats[:, :, m] for m in (1, 2, 4, 5))
                        gap = link(lambda: nc.vector.tensor_tensor(nt["gap"][:], mean_e, mean_o, ALU.subtract))
                        link(lambda: nc.vector.tensor_tensor(nt["sum"][:], mean_e, mean_o, ALU.add))
                        sq = link(lambda: nc.vector.tensor_tensor(nt["sq"][:], sq_e, sq_o, ALU.add))
                        reads(gap)
                        gap2 = link(lambda: nc.vector.tensor_tensor(nt["gap2"][:], nt["gap"][:], nt["gap"][:], ALU.mult))
                        reads(gap2)
                        sq_all = link(lambda: nc.vector.scalar_tensor_tensor(
                            out=nt["sq_all"][:], in0=nt["gap2"][:], scalar=F / 4, in1=nt["sq"][:], op0=ALU.mult, op1=ALU.add))
                        reads(sq_all)
                        nc.vector.tensor_scalar(nt["var"][:], nt["sq_all"][:], 1.0 / F, EPS, ALU.mult,
                                                ALU.add).then_inc(var_made, 1)
                        between(0)
                        between(1)
                        wait(dve, std_made, k.times(1, 1))
                        inv = link(lambda: nc.vector.reciprocal(nt["inv"][:], nt["std"][:]))
                        between(2)
                        reads(inv)
                        ratio = link(lambda: nc.vector.scalar_tensor_tensor(
                            out=nt["ratio"][:], in0=nt["inv"][:], scalar=-0.5, in1=nt["var"][:], op0=ALU.mult, op1=ALU.mult))
                        between(3)
                        reads(ratio)
                        step = link(lambda: nc.vector.tensor_tensor(nt["step"][:], nt["ratio"][:], nt["inv"][:], ALU.mult))
                        between(4)
                        reads(step)
                        scale = link(lambda: nc.vector.scalar_tensor_tensor(
                            out=rstd[:, h], in0=nt["step"][:], scalar=1.5, in1=nt["inv"][:], op0=ALU.add, op1=ALU.mult))
                        between(5)
                        reads(scale)
                        nc.vector.scalar_tensor_tensor(out=shift[:, h], in0=nt["sum"][:], scalar=-0.5,
                                                       in1=rstd[:, h], op0=ALU.mult,
                                                       op1=ALU.mult).then_inc(shift_made, 1)
                        assert n[0] == links

                    nc.vector.memset(line[96:CH, EP:EP + HALO], PAD_NODE).then_inc(line_set, 1)
                    nc.vector.memset(hs[:, :, :, ONE], 1.0).then_inc(hs_set, 1)
                    nc.vector.memset(ones[:], 1.0).then_inc(ones_made, 1)
                    nc.vector.memset(d3[:], 0.0).then_inc(split, 1)
                    nc.vector.memset(rel_all[:], -float(PAD_NODE)).then_inc(rows_kept, 1)
                    normal(Step(0))
                    dve.wait_ge(uv_summed, 1)
                    nc.vector.tensor_copy(uv_col[:].rearrange("p f s -> p (f s)"), uv_ps).then_inc(uv_kept, 1)
                    dve.wait_ge(uv_bc_summed, 1)
                    nc.vector.tensor_copy(uv_bc[:], uv_bc_ps[:]).then_inc(uv_bc_kept, 1)
                    dve.wait_ge(uv_bc_kept, 1)

                    def one(k):
                        wait(dve, dots_moved, k.times(1, 1))
                        if k.c + 1 < NS:
                            normal(k.plus(1), k)
                        for n in range(6 if k.c + 1 < NS else 0, 2 * ON_DVE):
                            dot(k, n // 2, n % 2)
                        wait(dve, dots_made, k.times(2 * ON_DVE, 2 * ON_DVE))
                        nc.vector.tensor_copy(d_all[:, bass.ds(k.times(NT, ON_PE), ON_DVE)],
                                              dots[:]).then_inc(dots_moved, 1)

                    dve.sem_inc(dots_moved, 1)
                    for k in range(NS):
                        if k == NS - 1:
                            edges()
                        one(Step(k))
                    dve.wait_ge(dots_free, NS + 1)
                    dve.wait_ge(dots_moved, NS + 1)
                    dve.wait_ge(bad_turned, 1)
                    nc.vector.tensor_reduce(bad_row[:, 0:1], bad_ps, AX.X, ALU.max).then_inc(bads, 1)
                    dve.wait_ge(bads, 4)
                    nc.vector.tensor_scalar(flag[:], bad_row[:, 0:1], 0.0, None, ALU.is_gt).then_inc(bads, 1)
                    high, mid, low_part = (d3[:, 1:NW + 1, k] for k in range(3))
                    for n, ins in enumerate((
                            lambda: nc.vector.tensor_copy(high, d_all[:]),
                            lambda: nc.vector.tensor_tensor(rest[:, 0], d_all[:], high, ALU.subtract),
                            lambda: nc.vector.tensor_copy(mid, rest[:, 0]),
                            lambda: nc.vector.tensor_tensor(rest[:, 1], rest[:, 0], mid, ALU.subtract),
                            lambda: nc.vector.tensor_copy(low_part, rest[:, 1]))):
                        dve.wait_ge(split, n + 1)
                        ins().then_inc(split, 1)

        shared = dict(locals())
        sorted_path(nc, shared)
        general_path(nc, shared)


def sorted_path(nc, g):
    x_all, d3, node_id, iota, ae_bc, WT, ident = (g[k] for k in (
        "x_all", "d3", "node_id", "iota", "ae_bc", "WT", "ident"))
    src_all, rel_all, flag = (g[k] for k in ("src_all", "rel_all", "flag"))
    table, dst_pad, dst16_pad, r_pad = (g[k] for k in ("table", "dst_pad", "dst16_pad", "r_pad"))
    FRONT_P = g["FRONT_P"]
    edge_attr, out = (g[k] for k in ("edge_attr", "out"))
    WN, CH, NW, NC, NB, G, F, FE, KF, ROW, S, FRONT = (g[k] for k in (
        "WN", "CH", "NW", "NC", "NB", "G", "F", "FE", "KF", "ROW", "S", "FRONT"))
    GE = G * CH
    WIDE = CH + 2 * HALO
    LEFT, RIGHT = SHARED + 1, SHARED - 1

    chunk_list = ([(-1, G - RIGHT + b) for b in range(RIGHT)] + [(0, b) for b in range(G)]
                  + [(1, b) for b in range(LEFT)])
    PER_WINDOW = len(chunk_list)
    parts = [range(0, 6), range(6, 12), range(12, 17), range(17, 22), range(22, PER_WINDOW)]
    EARLY = 4
    assert RIGHT + G == 22

    def in_window(w, n):
        kb, b = chunk_list[n]
        if w.i is not None:
            return True
        return 0 <= G * (w.c + kb) - 1 + b < NC

    with ExitStack() as ctx:
        def sb(name, shape, dt):
            return ctx.enter_context(nc.sbuf_tensor(name, shape, dt))

        def ps(name, shape):
            return ctx.enter_context(nc.psum_tensor(name, shape, F32))

        def sem(name):
            return ctx.enter_context(nc.semaphore(name))

        rows = sb("gathered_rows", [CH, UNROLL, G, ROW], F32)
        index = sb("index", [CH, UNROLL, G], I32)
        ef = sb("ef", [CH, 2, G, FE], F32)
        ef_a = sb("ef_a", [CH, G, FE], F32)
        ee = sb("ee", [CH, 2, G], F32)
        r = sb("r", [CH, 2, G], F32)
        r_row = sb("r_row", [G, 2, CH], F32)
        dst_bc = sb("dst_bc", [128, 2, GE], I16)
        is_dst = sb("is_dst", [WN, GE + (LEFT + RIGHT) * CH], BF16)
        d3_now = sb("d3_now", [WN, 2, 3, 3], BF16)
        d_dst = sb("d_dst", [CH, G], F32)
        dst_wide = sb("dst_wide", [G, 2, WIDE], I32)
        fall = sb("fall", [G, WIDE - 1], F32)
        cut = sb("cut", [G, 2, WIDE - 1], F32)
        r_wide = sb("r_wide", [G, 2, WIDE], F32)
        fwd = sb("fwd", [G, WIDE], F32)
        bwd = sb("bwd", [G, WIDE], F32)
        top = sb("top", [G, CH], F32)
        both = sb("both", [CH, 2, G], F32)
        leaky = sb("leaky", [CH, 2, G], F32)
        below = sb("below", [CH, G], F32)
        ex = sb("ex", [CH, 2, G], F32)
        rel = sb("rel", [CH, 2, G], F32)
        wts = sb("wts", [CH, PER_WINDOW, WN], F32)
        den = sb("den", [WN, 2], F32)
        agg = sb("agg", [WN, F], F32)
        aggT = sb("aggT", [128, KF, WN], F32)
        o = sb("o", [WN, 2, F], F32)
        acc = ps("acc", [WN, 2, 512])
        z_ps = ps("z_ps", [WN, F])
        aggT_ps = ps("aggT_ps", [128, KF, WN])
        d_ps = ps("d_ps", [CH, 2, 512])
        r_ps = ps("r_ps", [G, CH])
        both_ps = ps("both_ps", [CH, 2, G])

        loaded = [sem(f"loaded{h}") for h in range(2)]
        prepared = sem("prepared")
        index_made = sem("index_made")
        gathered = [sem(f"gathered{s}") for s in range(UNROLL)]
        slot_free = sem("slot_free")
        ef_a_made = sem("ef_a_made")
        ee_made = sem("ee_made")
        r_made = sem("r_made")
        r_turned = sem("r_turned")
        r_row_made = sem("r_row_made")
        r_out = [sem(f"r_out{h}") for h in range(2)]
        r_wide_in = [sem(f"r_wide_in{h}") for h in range(2)]
        is_dst_made = sem("is_dst_made")
        d_summed = sem("d_summed")
        d_kept = sem("d_kept")
        fall_made = sem("fall_made")
        scanned = sem("scanned")
        top_made = sem("top_made")
        both_turned = sem("both_turned")
        both_made = sem("both_made")
        leaky_made = sem("leaky_made")
        below_made = sem("below_made")
        ex_made = sem("ex_made")
        rel_kept = sem("rel_kept")
        wts_made = sem("wts_made")
        wts_used = sem("wts_used")
        den_made = sem("den_made")
        agg_made = sem("agg_made")
        agg_turned = sem("agg_turned")
        aggT_kept = sem("aggT_kept")
        z_made = sem("z_made")
        o_made = sem("o_made")
        stored = [sem(f"stored{h}") for h in range(2)]
        pool_at = sem("pool_at")
        pe_at = sem("pe_at")

        def steps(engine, one):
            turns = (NW - 2) // UNROLL - 1
            for c in range(UNROLL):
                one(Step(c))
            with engine.Fori(0, turns) as i:
                for c in range(UNROLL):
                    one(Step(UNROLL + c, i))
            for c in range(UNROLL + UNROLL * turns, NW + 2):
                one(Step(c))

        def has(k, d, n):
            return k.i is not None or 0 <= k.c + d < n

        def if_sorted(engine, body):
            bad = engine.value_load(flag[0:1, 0:1], min_val=0, max_val=1)
            with engine.If(bad == 0):
                body()
            with engine.Else():
                engine.nop()

        with nc.Block() as block:
            @block.sync
            def _(sp):
                def load(k):
                    h = k.c % 2
                    edges = k.times(GE)
                    wait(sp, prepared, k.times(1, -1))
                    if has(k, 0, NW):
                        for p, n in ((0, FRONT_P), (FRONT_P, CH - FRONT_P)):
                            sp.dma_start(ef[p:p + n, h], edge_attr[bass.ds(edges, GE), :].rearrange(
                                "(g p) c -> p g c", p=CH)[p:p + n]).then_inc(loaded[h], 16)
                    sp.dma_start(dst_bc[:, h], dst16_pad[bass.ds(edges, GE)].partition_broadcast(128)
                                 ).then_inc(loaded[h], 16)
                    sp.dma_start(dst_wide[:, h], wide_rows(dst_pad, k)).then_inc(loaded[h], 16)

                def wide_rows(padded, k):
                    at = padded[bass.ds(k.times(GE, FRONT - CH - HALO), (G - 1) * CH + WIDE)]
                    return bass.AP(tensor=at.tensor, offset=at.offset, ap=[[CH, G], [1, WIDE]])

                def one(k):
                    h = k.c % 2
                    if has(k, 2, NB):
                        load(k.plus(2))
                    if has(k, 0, NB):
                        wait(sp, both_turned, k.times(1, -1))
                        wait(sp, r_out[h], 16 * k.turns(2, 2) if has(k, 0, NW) else 0)
                        if not has(k, 0, NW):
                            sp.wait_ge(r_out[1 - h], 16 * k.turns(2, 1))
                        sp.dma_start(r_wide[:, h], wide_rows(r_pad, k)).then_inc(r_wide_in[h], 16)
                    if has(k, -2, NW):
                        w = k.plus(-2)
                        wait(sp, o_made, k.times(1, -1))
                        for p, n in ((0, FRONT_P), (FRONT_P, WN - FRONT_P)):
                            sp.dma_start(out[bass.ds(w.times(WN, p), n), :], o[p:p + n, h]).then_inc(stored[h], 16)

                def body():
                    load(Step(0))
                    load(Step(1))
                    steps(sp, one)
                    sp.wait_ge(stored[0], 32 * ((NW + 1) // 2))
                    sp.wait_ge(stored[1], 32 * (NW // 2))

                if_sorted(sp, body)

            @block.gpsimd
            def _(pool):
                def one(k):
                    s = k.c % UNROLL
                    if not has(k, 0, NW):
                        return
                    wait(pool, slot_free, k.times(1, 1))
                    wait(pool, index_made, k.times(1, 1))
                    pool.sem_inc(pool_at, 1)
                    for j in range(G):
                        pool.indirect_dma_start(out=rows[:, s, j, :],
                                                **on_row(table, index[:, s, j:j + 1])).then_inc(gathered[s], 16)

                def body():
                    pool.sem_inc(slot_free, UNROLL)
                    steps(pool, one)

                if_sorted(pool, body)

            @block.tensor
            def _(pe):
                def targets(k):
                    h = k.c % 2
                    wait(pe, is_dst_made, k.times(1, 1))
                    wait(pe, d_kept, k.times(1, -1))
                    here = [b for b in range(G) if k.i is not None or k.c < 2 or G * k.c - 1 + b < NC]
                    for b in here:
                        hot = [(is_dst[:, CH * b:CH * b + CH], 1)]
                        if b < LEFT:
                            hot.append((is_dst[:, GE + CH * b:GE + CH * b + CH], 0))
                        if b >= G - RIGHT:
                            at = GE + CH * (LEFT + b - (G - RIGHT))
                            hot.append((is_dst[:, at:at + CH], 2))
                        for n, (one_hot, w) in enumerate(hot):
                            mm = nc.tensor.matmul(d_ps[:, h, 3 * b:3 * b + 3], one_hot, d3_now[:, h, w, :],
                                                  start=(n == 0), stop=(n == len(hot) - 1))
                    mm.then_inc(d_summed, 1)

                def sums(w, part):
                    mine = [n for n in parts[part] if in_window(w, n)]
                    if mine:
                        wait(pe, wts_made, w.times(5, part))
                    first = next(n for n in range(PER_WINDOW) if in_window(w, n))
                    last = max(n for n in range(PER_WINDOW) if in_window(w, n))
                    for n in mine:
                        kb, b = chunk_list[n]
                        chunk = G * (w.c + kb) - 1 + b
                        mm = nc.tensor.matmul(acc[:, w.c % 2, 0:F + 1], wts[:, n, :],
                                              rows[:, chunk // G % UNROLL, chunk % G, 0:F + 1],
                                              start=(n == first), stop=(n == last))
                    if mine:
                        mm.then_inc(wts_used, 1)
                    if part == 0 and mine:
                        pe.wait_ge(wts_used, w.times(5, 0))
                        pe.sem_inc(slot_free, 1)

                def one(k):
                    w = k.plus(-1)
                    if has(k, 0, NW):
                        wait(pe, r_made, k.times(1, 1))
                        wait(pe, r_row_made, k.times(1))
                        nc.tensor.transpose(r_ps[:], r[:, k.c % 2, :], ident[0:CH, 0:CH]).then_inc(r_turned, 1)
                    if has(k, -1, NW):
                        wait(pe, agg_made, k.times(1, -2))
                        sums(w, 0)
                    if has(k, -2, NW):
                        wait(pe, agg_made, k.times(1, -1))
                        wait(pe, aggT_kept, k.times(1, -2))
                        for c in range(KF):
                            mm = nc.tensor.transpose(aggT_ps[:, c, :], agg[:, 128 * c:128 * c + 128],
                                                     ident[0:WN, 0:WN])
                        mm.then_inc(agg_turned, 1)
                    if has(k, -1, NW):
                        sums(w, 1)
                    if has(k, -2, NW):
                        wait(pe, aggT_kept, k.times(1, -1))
                        wait(pe, o_made, k.times(1, -2))
                        for c in range(KF):
                            mm = nc.tensor.matmul(z_ps[:], aggT[:, c, :], WT[:, c, :], start=(c == 0),
                                                  stop=(c == KF - 1))
                        mm.then_inc(z_made, 1)
                    if has(k, 1, NB):
                        targets(k.plus(1))
                    late = 2 if k.i is not None or k.c < NB - 2 else 3
                    if has(k, -1, NW) and late == 3:
                        sums(w, 2)
                    if has(k, 0, NB):
                        wait(pe, top_made, k.times(1, 1))
                        wait(pe, both_made, k.times(1))
                        pe.sem_inc(pe_at, 1)
                        nc.tensor.transpose(both_ps[:, 0, :], r_wide[:, k.c % 2, HALO:HALO + CH], ident[0:G, 0:G])
                        nc.tensor.transpose(both_ps[:, 1, :], top[:], ident[0:G, 0:G]).then_inc(both_turned, 1)
                    if has(k, -1, NW):
                        for part in range(late, 5):
                            sums(w, part)

                def body():
                    targets(Step(0))
                    steps(pe, one)

                if_sorted(pe, body)

            @block.scalar
            def _(act):
                def indices(k):
                    nc.scalar.copy(index[:, k.c % UNROLL, :], src_all[:, bass.ds(k.times(G), G)]).then_inc(index_made, 1)

                def one(k):
                    h = k.c % 2
                    if has(k, 2, NW):
                        indices(k.plus(2))
                    if has(k, 0, NW):
                        wait(act, r_turned, k.times(1, 1))
                        wait(act, r_out[h], 16 * k.turns(2))
                        nc.scalar.copy(r_row[:, h, :], r_ps[:]).then_inc(r_row_made, 1)
                        wait(act, r_row_made, k.times(1, 1))
                        act.dma_start(r_pad[bass.ds(k.times(GE, FRONT), GE)].rearrange("(g p) -> g p", p=CH),
                                      r_row[:, h, :]).then_inc(r_out[h], 16)
                    if has(k, -2, NW):
                        wait(act, den_made, k.times(2, -2))
                        wait(act, agg_turned, k.times(1, -2))
                        nc.scalar.mul(agg[:], acc[:, h, 0:F], den[:, 1:2]).then_inc(agg_made, 1)
                        wait(act, agg_turned, k.times(1, -1))
                        wait(act, z_made, k.times(1, -2))
                        nc.scalar.copy(aggT[:].rearrange("p k n -> p (k n)"),
                                       aggT_ps[:].rearrange("p k n -> p (k n)")).then_inc(aggT_kept, 1)
                    if has(k, 0, NB):
                        wait(act, below_made, k.times(1, 1))
                        nc.scalar.activation(ex[:, h, :], below[:], ACT.Exp).then_inc(ex_made, 1)

                def body():
                    indices(Step(0))
                    indices(Step(1))
                    steps(act, one)

                if_sorted(act, body)

            @block.vector
            def _(dve):
                def prepare(k):
                    h = k.c % 2
                    n_loads = 4
                    if has(k, 0, NW):
                        dve.wait_ge(loaded[h], 16 * n_loads * k.turns(2, 2) if k.i is None
                                    else 16 * n_loads * k.turns(2, 2))
                    else:
                        dve.wait_ge(loaded[h], 16 * (n_loads * k.turns(2) + 2))
                    wait(dve, d_summed, k.times(1))
                    for to, of, w in ((slice(0, GE), slice(0, GE), 1),
                                      (slice(GE, GE + LEFT * CH), slice(0, LEFT * CH), 0),
                                      (slice(GE + LEFT * CH, None), slice(GE - RIGHT * CH, GE), 2)):
                        nc.vector.tensor_scalar(is_dst[:, to], dst_bc[0:WN, h, of],
                                                node_id[:, bass.ds(k.times(1, w), 1)], None, ALU.is_equal)
                    nc.vector.tensor_copy(d3_now[:, h], d3[:, bass.ds(k.times(1), 3), :]).then_inc(is_dst_made, 1)
                    wait(dve, fall_made, k.times(2))
                    nc.vector.tensor_tensor(fall[:], dst_wide[:, h, 0:WIDE - 1], dst_wide[:, h, 1:WIDE],
                                            ALU.subtract).then_inc(fall_made, 1)
                    if has(k, 0, NW):
                        nc.vector.tensor_tensor(ef_a[:], ef[:, h], ae_bc[:].unsqueeze(1).broadcast_to([CH, G, FE]),
                                                ALU.mult).then_inc(ef_a_made, 1)
                    dve.wait_ge(fall_made, k.times(2, 1))
                    nc.vector.tensor_scalar(cut[:, h, :], fall[:], BIG, None, ALU.mult).then_inc(fall_made, 1)
                    if has(k, 0, NW):
                        dve.wait_ge(ef_a_made, k.times(1, 1))
                        nc.vector.tensor_reduce(ee[:, h, :], ef_a[:], AX.X, ALU.add).then_inc(ee_made, 1)
                    dve.wait_ge(fall_made, k.times(2, 2))
                    dve.sem_inc(prepared, 1)

                def weights(w, part):
                    mine = [n for n in parts[part] if in_window(w, n)]
                    if not mine:
                        return
                    wait(dve, wts_used, w.times(5, part - 5) if w.i is not None or w.c else 0)
                    for n in mine:
                        kb, b = chunk_list[n]
                        h = (w.c + kb) % 2
                        at = WN * (1 - kb)
                        ins = nc.vector.tensor_scalar(wts[:, n, :], iota[:, at:at + WN], rel[:, h, b:b + 1],
                                                      ex[:, h, b:b + 1], ALU.is_equal, ALU.mult)
                    ins.then_inc(wts_made, 1)

                def one(k):
                    h = k.c % 2
                    if has(k, 0, NW):
                        s = k.c % UNROLL
                        dve.wait_ge(gathered[s], 16 * G * k.turns(UNROLL, UNROLL))
                        dve.wait_ge(ee_made, k.times(1, 1))
                        nc.vector.tensor_tensor(r[:, h, :], rows[:, s, :, S], ee[:, h, :], ALU.add).then_inc(r_made, 1)
                    if has(k, -2, NW):
                        dve.wait_ge(wts_used, k.times(5, -6))
                        nc.vector.tensor_scalar(den[:, 0:1], acc[:, h, F:F + 1], TINY, None, ALU.max).then_inc(den_made, 1)
                        dve.wait_ge(den_made, k.times(2, -3))
                        nc.vector.reciprocal(den[:, 1:2], den[:, 0:1]).then_inc(den_made, 1)
                    if has(k, 1, NB):
                        prepare(k.plus(1))
                    if has(k, 0, NB):
                        dve.wait_ge(d_summed, k.times(1, 1))
                        nc.vector.tensor_reduce(d_dst[:], d_ps[:, h, 0:3 * G].rearrange("p (g c) -> p g c", c=3), AX.X, ALU.add).then_inc(d_kept, 1)
                        wait(dve, wts_made, k.times(5, -2))
                        nc.vector.tensor_copy(rel[:, h, :], rel_all[:, bass.ds(k.times(G), G)]).then_inc(rel_kept, 1)
                    if has(k, -2, NW):
                        dve.wait_ge(z_made, k.times(1, -1))
                        wait(dve, stored[h], 32 * k.turns(2, -2))
                        nc.vector.tensor_tensor(o[:, h, :], z_ps[:], x_all[:, bass.ds(k.times(1, -2), 1), :]
                                                .rearrange("p a f -> p (a f)"), ALU.add).then_inc(o_made, 1)
                    if has(k, 0, NB):
                        dve.wait_ge(r_wide_in[h], 16 * k.turns(2, 2))
                        nc.vector.tensor_tensor_scan(fwd[:, 1:HALO + CH], cut[:, h, 0:HALO + CH - 1],
                                                     r_wide[:, h, 1:HALO + CH], -BIG, ALU.add, ALU.max)
                        nc.vector.tensor_tensor_scan(bwd[:, WIDE - 2:HALO - 1:-1], cut[:, h, WIDE - 2:HALO - 1:-1],
                                                     r_wide[:, h, WIDE - 2:HALO - 1:-1], -BIG, ALU.add,
                                                     ALU.max).then_inc(scanned, 1)
                        dve.wait_ge(scanned, k.times(1, 1))
                        nc.vector.tensor_tensor(top[:], fwd[:, HALO:HALO + CH], bwd[:, HALO:HALO + CH],
                                                ALU.max).then_inc(top_made, 1)
                        dve.wait_ge(both_turned, k.times(1, 1))
                        dve.wait_ge(d_kept, k.times(1, 1))
                        nc.vector.tensor_tensor(both[:], both_ps[:], d_dst[:].unsqueeze(1).broadcast_to([CH, 2, G]),
                                                ALU.add).then_inc(both_made, 1)
                        dve.wait_ge(both_made, k.times(1, 1))
                        nc.vector.scalar_tensor_tensor(out=leaky[:], in0=both[:], scalar=SLOPE, in1=both[:],
                                                       op0=ALU.mult, op1=ALU.max).then_inc(leaky_made, 1)
                        dve.wait_ge(leaky_made, k.times(1, 1))
                        nc.vector.tensor_tensor(below[:], leaky[:, 0], leaky[:, 1], ALU.subtract).then_inc(below_made, 1)
                        dve.wait_ge(ex_made, k.times(1, 1))
                        dve.wait_ge(rel_kept, k.times(1, 1))
                    if has(k, -1, NW):
                        weights(k.plus(-1), EARLY)
                    if has(k, 0, NW):
                        for part in range(EARLY):
                            weights(k, part)

                def body():
                    prepare(Step(0))
                    steps(dve, one)

                if_sorted(dve, body)


def general_path(nc, g):
    x_all, d_all, ae_bc, WT, ident, flag = (g[k] for k in ("x_all", "d_all", "ae_bc", "WT", "ident", "flag"))
    table, state, src, dst, edge_attr, out = (g[k] for k in ("table", "state", "src", "dst", "edge_attr", "out"))
    S, WN, CH, NW, NC, F, FE, KF, ROW, ST, N = (g[k] for k in ("S", "WN", "CH", "NW", "NC", "F", "FE", "KF", "ROW", "ST", "N"))
    DEN, MAX, DCOL = F, F + 1, F + 2
    with ExitStack() as ctx:
        def sb(name, shape, dt):
            return ctx.enter_context(nc.sbuf_tensor(name, shape, dt))

        def ps(name, shape):
            return ctx.enter_context(nc.psum_tensor(name, shape, F32))

        def sem(name):
            return ctx.enter_context(nc.semaphore(name))

        first = sb("first", [WN, 10, ST], F32)
        later = sb("later", [CH, CH], F32)
        ones = sb("g_ones", [CH, CH], F32)
        si = sb("si", [CH, 1], I32)
        di = sb("di", [CH, 1], I32)
        ef = sb("g_ef", [CH, FE], F32)
        efj = sb("g_efj", [CH, FE], F32)
        hg = sb("hg", [CH, ROW], F32)
        sg = sb("sg", [CH, ST], F32)
        sn = sb("sn", [CH, ST], F32)
        col = sb("col", [CH, 8], F32)
        arg = sb("arg", [CH, 2], F32)
        ex = sb("g_ex", [CH, 2], F32)
        rep = sb("rep", [CH, 2, CH], F32)
        row = sb("row", [CH, 2, CH], F32)
        eq = sb("eq", [CH, CH], F32)
        m1 = sb("m1", [CH, CH], F32)
        m2 = sb("m2", [CH, CH], F32)
        wt = sb("g_wt", [CH, CH], F32)
        dup = sb("dup", [CH, CH], F32)
        so = sb("so", [CH, 1], I32)
        row_ps = ps("row_ps", [CH, 2, CH])
        sum_ps = ps("sum_ps", [CH, F + 1])
        st = sb("st", [WN, ST], F32)
        rden = sb("g_rden", [WN, 2], F32)
        agg = sb("g_agg", [WN, F], F32)
        aggT = sb("g_aggT", [128, KF, WN], F32)
        ob = sb("g_ob", [WN, F], F32)
        aggT_ps = ps("g_aggT_ps", [128, KF, WN])
        z_ps = ps("g_z_ps", [WN, F])

        made = sem("g_made")
        first_out = sem("g_first_out")
        loaded = sem("g_loaded")
        gathered = sem("g_gathered")
        rows_turned = sem("g_rows_turned")
        rep_made = sem("g_rep_made")
        first_ready = sem("g_first_ready")
        arg_made = sem("g_arg_made")
        ex_made = sem("g_ex_made")
        wt_made = sem("g_wt_made")
        summed = sem("g_summed")
        v = sem("g_v")
        new_state = sem("g_new_state")
        scattered = sem("g_scattered")
        state_in = sem("g_state_in")
        agg_made = sem("g_agg_made")
        agg_turned = sem("g_agg_turned")
        aggT_kept = sem("g_aggT_kept")
        z_made = sem("g_z_made")
        den_made = sem("g_den_made")
        ob_made = sem("g_ob_made")
        pool_at = sem("g_pool_at")
        stored = sem("g_stored")

        chunk_ops = 14
        def if_unsorted(engine, body):
            bad = engine.value_load(flag[0:1, 0:1], min_val=0, max_val=1)
            with engine.If(bad == 1):
                body()
            with engine.Else():
                engine.nop()

        with nc.Block() as block:
            @block.sync
            def _(sp):
                def body():
                    sp.sem_inc(first_out, 16)
                    with sp.Fori(0, 5) as b:
                        sp.wait_ge(first_ready, b + 1)
                        sp.dma_start(state.rearrange("(t p) f -> p t f", p=WN)[:, bass.ds(10 * b, 10), :],
                                     first[:]).then_inc(first_out, 16)
                    sp.wait_ge(first_out, 16 * 6)
                    def load(c):
                        sp.dma_start(si[:], src[bass.ds(CH * c, CH)].rearrange("(p a) -> p a", a=1)).then_inc(loaded, 16)
                        sp.dma_start(di[:], dst[bass.ds(CH * c, CH)].rearrange("(p a) -> p a", a=1)).then_inc(loaded, 16)
                        sp.dma_start(ef[:], edge_attr[bass.ds(CH * c, CH), :]).then_inc(loaded, 16)

                    load(0)
                    with sp.Fori(1, NC) as c:
                        sp.wait_ge(scattered, 16 * c)
                        load(c)
                    sp.sem_inc(stored, 16)
                    sp.sem_inc(ob_made, 1)
                    sp.wait_ge(scattered, 16 * NC)
                    with sp.Fori(0, NW) as w:
                        sp.wait_ge(ob_made, w + 1)
                        sp.dma_start(st[:], state[bass.ds(WN * w, WN), :]).then_inc(state_in, 16)
                        sp.wait_ge(ob_made, w + 2)
                        sp.dma_start(out[bass.ds(WN * w, WN), :], ob[:]).then_inc(stored, 16)
                    sp.wait_ge(stored, 16 * NW + 16)

                if_unsorted(sp, body)

            @block.gpsimd
            def _(pool):
                def body():
                    nc.gpsimd.memset(later[:], 1.0).then_inc(made, 1)
                    pool.wait_ge(made, 1)
                    nc.gpsimd.affine_select(out=later[:], in_=later[:], compare_op=ALU.is_gt, fill=0.0, base=0,
                                            pattern=[[1, CH]], channel_multiplier=-1).then_inc(made, 1)
                    pool.wait_ge(first_out, 16 * 6)
                    with pool.Fori(0, NC) as c:
                        pool.wait_ge(loaded, 48 * c + 48)
                        pool.sem_inc(pool_at, 1)
                        pool.indirect_dma_start(out=hg[:], **on_row(table, si[:])).then_inc(gathered, 16)
                        pool.indirect_dma_start(out=sg[:], **on_row(state, di[:])).then_inc(gathered, 16)
                        pool.wait_ge(new_state, 4 * c + 4)
                        pool.sem_inc(pool_at, 1)
                        pool.indirect_dma_start(out=state, out_offset=bass.IndirectOffsetOnAxis(ap=so[:], axis=0),
                                                in_=sn[:], in_offset=None, bounds_check=N - 1,
                                                oob_is_err=False).then_inc(scattered, 16)

                if_unsorted(pool, body)

            @block.tensor
            def _(pe):
                def body():
                    with pe.Fori(0, NC) as c:
                        pe.wait_ge(rep_made, 2 * c + 2)
                        for s in range(2):
                            mm = nc.tensor.transpose(row_ps[:, s, :], rep[:, s, :], ident[0:CH, 0:CH])
                        mm.then_inc(rows_turned, 1)
                        pe.wait_ge(wt_made, c + 1)
                        nc.tensor.matmul(sum_ps[:], wt[:], hg[:, 0:F + 1], start=True, stop=True).then_inc(summed, 1)
                    with pe.Fori(0, NW) as w:
                        pe.wait_ge(agg_made, w + 1)
                        for k in range(KF):
                            mm = nc.tensor.transpose(aggT_ps[:, k, :], agg[:, 128 * k:128 * k + 128], ident[0:WN, 0:WN])
                        mm.then_inc(agg_turned, 1)
                        pe.wait_ge(aggT_kept, w + 1)
                        for k in range(KF):
                            mm = nc.tensor.matmul(z_ps[:], aggT[:, k, :], WT[:, k, :], start=(k == 0), stop=(k == KF - 1))
                        mm.then_inc(z_made, 1)

                if_unsorted(pe, body)

            @block.scalar
            def _(act):
                def body():
                    with act.Fori(0, NC) as c:
                        act.wait_ge(arg_made, 2 * c + 2)
                        nc.scalar.activation(ex[:], arg[:], ACT.Exp).then_inc(ex_made, 1)
                    with act.Fori(0, NW) as w:
                        act.wait_ge(agg_turned, w + 1)
                        nc.scalar.copy(aggT[:].rearrange("p k n -> p (k n)"),
                                       aggT_ps[:].rearrange("p k n -> p (k n)")).then_inc(aggT_kept, 1)

                if_unsorted(act, body)

            @block.vector
            def _(dve):
                def body():
                    nc.vector.memset(ones[:], 1.0).then_inc(v, 1)
                    nc.vector.memset(first[:], 0.0).then_inc(v, 1)
                    dve.wait_ge(v, 2)
                    nc.vector.memset(first[:, :, MAX], -BIG).then_inc(v, 1)
                    dve.wait_ge(v, 3)
                    dve.wait_ge(made, 2)
                    with dve.Fori(0, 5) as b:
                        dve.wait_ge(first_out, 16 * b + 16)
                        nc.vector.tensor_copy(first[:, :, DCOL], d_all[:, bass.ds(10 * b, 10)]).then_inc(first_ready, 1)
                    with dve.Fori(0, NC) as c:
                        n = [3]

                        def then(ins):
                            n[0] += 1
                            ins.then_inc(v, 1)
                            dve.wait_ge(v, chunk_ops * c + n[0])

                        dstf, ee, r, lg, l, mx, m_new, twice = (col[:, i:i + 1] for i in range(8))
                        dve.wait_ge(loaded, 48 * c + 48)
                        dve.wait_ge(gathered, 32 * c + 32)
                        then(nc.vector.tensor_copy(dstf, di[:]))
                        then(nc.vector.tensor_tensor_reduce(efj[:], ef[:], ae_bc[:], 1.0, 0.0, ALU.mult, ALU.add, ee))
                        then(nc.vector.tensor_tensor(r, ee, hg[:, S:S + 1], ALU.add))
                        then(nc.vector.tensor_tensor(lg, r, sg[:, DCOL:DCOL + 1], ALU.add))
                        then(nc.vector.scalar_tensor_tensor(out=l, in0=lg, scalar=SLOPE, in1=lg, op0=ALU.mult,
                                                            op1=ALU.max))
                        nc.vector.tensor_scalar(rep[:, 0, :], ones[:], dstf, None, ALU.mult).then_inc(rep_made, 1)
                        nc.vector.tensor_scalar(rep[:, 1, :], ones[:], l, None, ALU.mult).then_inc(rep_made, 1)
                        dve.wait_ge(rows_turned, c + 1)
                        then(nc.vector.tensor_copy(row[:], row_ps[:]))
                        then(nc.vector.tensor_scalar(eq[:], row[:, 0, :], dstf, None, ALU.is_equal))
                        then(nc.vector.tensor_scalar(m1[:], eq[:], -1.0, BIG, ALU.add, ALU.mult))
                        then(nc.vector.tensor_tensor(m2[:], m1[:], row[:, 1, :], ALU.add))
                        then(nc.vector.tensor_reduce(mx, m2[:], AX.X, ALU.max))
                        then(nc.vector.tensor_tensor(m_new, mx, sg[:, MAX:MAX + 1], ALU.max))
                        nc.vector.tensor_tensor(arg[:, 0:1], l, m_new, ALU.subtract).then_inc(arg_made, 1)
                        nc.vector.tensor_tensor(arg[:, 1:2], sg[:, MAX:MAX + 1], m_new, ALU.subtract).then_inc(arg_made, 1)
                        then(nc.vector.tensor_tensor(dup[:], eq[:], later[:], ALU.mult))
                        then(nc.vector.tensor_reduce(twice, dup[:], AX.X, ALU.max))
                        nc.vector.scalar_tensor_tensor(out=so[:], in0=twice, scalar=float(2 * N), in1=dstf,
                                                       op0=ALU.mult, op1=ALU.add).then_inc(new_state, 1)
                        nc.vector.tensor_copy(sn[:, MAX:MAX + 1], m_new).then_inc(new_state, 1)
                        nc.vector.tensor_copy(sn[:, DCOL:DCOL + 1], sg[:, DCOL:DCOL + 1]).then_inc(new_state, 1)
                        dve.wait_ge(ex_made, c + 1)
                        nc.vector.tensor_scalar(wt[:], eq[:], ex[:, 0:1], None, ALU.mult).then_inc(wt_made, 1)
                        dve.wait_ge(summed, c + 1)
                        then(nc.vector.scalar_tensor_tensor(out=sn[:, 0:F + 1], in0=sg[:, 0:F + 1], scalar=ex[:, 1:2],
                                                            in1=sum_ps[:], op0=ALU.mult, op1=ALU.add))
                        nc.vector.sem_inc(new_state, 1)
                        assert n[0] == chunk_ops + 3
                    with dve.Fori(0, NW) as w:
                        dve.wait_ge(state_in, 16 * w + 16)
                        nc.vector.tensor_scalar(rden[:, 0:1], st[:, DEN:DEN + 1], TINY, None,
                                                ALU.max).then_inc(den_made, 1)
                        dve.wait_ge(den_made, 2 * w + 1)
                        nc.vector.reciprocal(rden[:, 1:2], rden[:, 0:1]).then_inc(den_made, 1)
                        dve.wait_ge(den_made, 2 * w + 2)
                        nc.vector.tensor_scalar(agg[:], st[:, 0:F], rden[:, 1:2], None, ALU.mult).then_inc(agg_made, 1)
                        dve.wait_ge(z_made, w + 1)
                        dve.wait_ge(stored, 16 * w + 16)
                        nc.vector.tensor_tensor(ob[:], z_ps[:], x_all[:, bass.ds(w, 1), :].rearrange("p a f -> p (a f)"),
                                                ALU.add).then_inc(ob_made, 1)

                if_unsorted(dve, body)


def kernel(x, src, dst, edge_attr_64, L0_gnn_W, L0_gnn_A):
    import numpy as np
    import concourse.bacc as bacc
    from concourse.bass_utils import run_bass_kernel_spmd

    nc = bacc.Bacc("TRN2", target_bir_lowering=False, num_devices=1)
    given = {"x": x, "src": src, "dst": dst, "edge_attr": edge_attr_64, "W": L0_gnn_W, "A": L0_gnn_A}
    arrays, aps = {}, {}
    for name, a in given.items():
        a = np.ascontiguousarray(a)
        arrays[f"in_{name}"] = a
        aps[name] = nc.dram_tensor(f"in_{name}", a.shape, mybir.dt.from_np(a.dtype), kind="ExternalInput").ap()
    aps["out"] = nc.dram_tensor("out", tuple(x.shape), F32, kind="ExternalOutput").ap()
    gnn_kernel(nc, **aps)
    return run_bass_kernel_spmd(nc, [arrays], core_ids=[0]).results[0]["out"]
```
